# Optimizing a Trainium2 kernel written in Bass

```python
import numpy as np
import jax
import jax.numpy as jnp

def _softmax(x, axis=-1):
    return jax.nn.softmax(x, axis=axis)
def _gelu(x):
    return jax.nn.gelu(x, approximate=True)
def _silu(x):
    return jax.nn.silu(x)
def _sigmoid(x):
    return jax.nn.sigmoid(x)
def _layernorm(x, axis=-1, eps=1e-5):
    m = jnp.mean(x, axis=axis, keepdims=True)
    v = jnp.var(x, axis=axis, keepdims=True)
    return (x - m) / jnp.sqrt(v + eps)
def _scatter_add(tgt, idx, src, axis=0):
    return tgt.at[idx].add(src)
def _segment_sum(src, seg, n):
    return jax.ops.segment_sum(src, seg, n)

kernel_name = 'mk_conv_attn_hybrid_d2_conv_nchw128_9fc154'

def setup_inputs(seed: int = 0):
    np.random.seed(seed)
    _w = jnp.asarray
    def _rec_inputs():
        import jax
        import jax.numpy as jnp
        _gk = jax.random.key(seed)
        x = -0.0005207 + 1.001 * jax.random.normal(jax.random.fold_in(_gk, 1), (4, 128, 64, 64), jnp.float32)
        return x
    x = _rec_inputs()
    def _L0_conv_setup():
        import jax, jax.numpy as jnp
        import numpy as np
        from jax import lax
        IN_C = 128
        OUT_C = 128
        K = 3
        STRIDE = 1
        PAD = 1
        N, H, W = (4, 64, 64)

        def _dcn_forward(x, offset_w, offset_b, dcn_w):
            n, in_c, h, w = x.shape
            out_c, _, kh, kw = dcn_w.shape
            kk = kh * kw
            f32 = x.dtype
            om = lax.conv_general_dilated(x, offset_w, (STRIDE, STRIDE), [(PAD, PAD), (PAD, PAD)], dimension_numbers=('NCHW', 'OIHW', 'NCHW')) + offset_b[None, :, None, None]
            off_y = jnp.transpose(om[:, 0:2 * kk:2], (0, 2, 3, 1))
            off_x = jnp.transpose(om[:, 1:2 * kk:2], (0, 2, 3, 1))
            mask = jax.nn.sigmoid(jnp.transpose(om[:, 2 * kk:], (0, 2, 3, 1)))
            out_h = (h + 2 * PAD - (kh - 1)) // STRIDE
            out_w = (w + 2 * PAD - (kw - 1)) // STRIDE
            pad_x = jnp.pad(x, ((0, 0), (0, 0), (PAD, PAD + 1), (PAD, PAD + 1)))
            pad_x = jnp.transpose(pad_x, (0, 2, 3, 1))
            base_y = (jnp.arange(out_h, dtype=f32) * STRIDE + PAD)[None, :, None, None]
            base_x = (jnp.arange(out_w, dtype=f32) * STRIDE + PAD)[None, None, :, None]
            half = (kw - 1) // 2
            inner_y = jnp.repeat(jnp.arange(kh, dtype=f32) - half, kw)
            inner_x = jnp.tile(jnp.arange(kw, dtype=f32) - half, kh)
            pos_y = jnp.clip(base_y + inner_y + off_y, 0.0, h + 2 * PAD - 1.0)
            pos_x = jnp.clip(base_x + inner_x + off_x, 0.0, w + 2 * PAD - 1.0)
            y1 = jnp.floor(pos_y)
            x1 = jnp.floor(pos_x)
            y1i = y1.astype(jnp.int32)
            x1i = x1.astype(jnp.int32)
            y2i = y1i + 1
            x2i = x1i + 1
            n_idx = jnp.arange(n)[:, None, None, None]
            v1 = pad_x[n_idx, y1i, x1i]
            v2 = pad_x[n_idx, y1i, x2i]
            v3 = pad_x[n_idx, y2i, x1i]
            v4 = pad_x[n_idx, y2i, x2i]
            lh = (pos_y - y1)[..., None]
            lw = (pos_x - x1)[..., None]
            hh = 1.0 - lh
            hw = 1.0 - lw
            value = (hh * hw * v1 + hh * lw * v2 + lh * hw * v3 + lh * lw * v4) * mask[..., None]
            out = jnp.einsum('nhwkc,ock->nohw', value, dcn_w.reshape(out_c, in_c, kk))
            return out
        key = jax.random.key(seed)
        k1, k2, k3 = jax.random.split(key, 3)
        x = jax.random.normal(k1, (N, IN_C, H, W), jnp.float32)
        offset_w = jax.random.normal(k2, (3 * K * K, IN_C, K, K), jnp.float32) * 0.01
        offset_b = jnp.zeros((3 * K * K,), jnp.float32)
        dcn_w = jax.random.normal(k3, (OUT_C, IN_C, K, K), jnp.float32) * (1.0 / np.sqrt(IN_C * K * K))
        return {'x': x, 'offset_w': offset_w, 'offset_b': offset_b, 'dcn_w': dcn_w}
    _L0_conv_all = _L0_conv_setup()
    _L0_conv_in = {k: v for k, v in _L0_conv_all.items() if k in ('offset_w', 'offset_b', 'dcn_w', )}
    del _L0_conv_all

    def _L1_attn_setup():
        import jax, jax.numpy as jnp
        import numpy as np
        B, S, H, D = (8, 1024, 16, 8)
        E, FFN = (H * D, 512)
        NQ_FFN = 8
        EPS = 1e-05

        def _qz_ring(phi):
            c = jnp.cos(phi)
            P = jnp.cumprod(c, axis=-1)
            z0 = jnp.prod(c[..., 1:], axis=-1, keepdims=True)
            return jnp.concatenate([z0, P[..., 1:]], axis=-1)

        def _ln(v, g, b):
            mu = jnp.mean(v, axis=-1, keepdims=True)
            var = jnp.mean((v - mu) ** 2, axis=-1, keepdims=True)
            return (v - mu) * jax.lax.rsqrt(var + EPS) * g + b
        key = jax.random.key(seed)
        ks = jax.random.split(key, 8)
        inp = {'x': jax.random.normal(ks[0], (B, S, E), jnp.float32), 'rx_theta': jax.random.normal(ks[1], (D,), jnp.float32), 'ry_theta': jax.random.normal(ks[2], (NQ_FFN,), jnp.float32), 'w_comb': jax.random.normal(ks[3], (E, E), jnp.float32) / np.sqrt(E), 'b_comb': jnp.zeros((E,), jnp.float32), 'w1': jax.random.normal(ks[4], (FFN, NQ_FFN), jnp.float32) / np.sqrt(NQ_FFN), 'b1': jnp.zeros((FFN,), jnp.float32), 'w2': jax.random.normal(ks[5], (E, FFN), jnp.float32) / np.sqrt(FFN), 'b2': jnp.zeros((E,), jnp.float32), 'g1': jnp.ones((E,), jnp.float32), 'beta1': jnp.zeros((E,), jnp.float32), 'g2': jnp.ones((E,), jnp.float32), 'beta2': jnp.zeros((E,), jnp.float32)}
        return inp
    _L1_attn_all = _L1_attn_setup()
    _L1_attn_in = {k: v for k, v in _L1_attn_all.items() if k in ('rx_theta', 'ry_theta', 'w_comb', 'b_comb', 'w1', 'b1', 'w2', 'b2', 'g1', 'beta1', 'g2', 'beta2', )}
    del _L1_attn_all

    def _L1_ffn_setup():
        import jax, jax.numpy as jnp
        import numpy as np
        B, S, D, E, H, O, K = (512, 2048, 128, 64, 512, 128, 8)
        key = jax.random.key(seed)
        k0, k1, k2, k3 = jax.random.split(key, 4)
        x = jax.random.normal(k0, (B, S, D), dtype=jnp.float32)
        gate_w = jax.random.normal(k1, (E, D), dtype=jnp.float32) * (1.0 / np.sqrt(D))
        gate_b = jnp.zeros((E,), dtype=jnp.float32)
        weight1 = jax.random.uniform(k2, (E, D + 1, H), dtype=jnp.float32, minval=-1.0, maxval=1.0) * (1.0 / np.sqrt(D + 1))
        weight2 = jax.random.uniform(k3, (E, H + 1, O), dtype=jnp.float32, minval=-1.0, maxval=1.0) * (1.0 / np.sqrt(H + 1))
        return {'x': x, 'gate_w': gate_w, 'gate_b': gate_b, 'weight1': weight1, 'weight2': weight2}
    _L1_ffn_all = _L1_ffn_setup()
    _L1_ffn_in = {k: v for k, v in _L1_ffn_all.items() if k in ('gate_w', 'gate_b', 'weight1', 'weight2', )}
    del _L1_ffn_all

    return {
        "x": x,
        "L0_conv_offset_w": _L0_conv_in["offset_w"],
        "L0_conv_offset_b": _L0_conv_in["offset_b"],
        "L0_conv_dcn_w": _L0_conv_in["dcn_w"],
        "L1_attn_rx_theta": _L1_attn_in["rx_theta"],
        "L1_attn_ry_theta": _L1_attn_in["ry_theta"],
        "L1_attn_w_comb": _L1_attn_in["w_comb"],
        "L1_attn_b_comb": _L1_attn_in["b_comb"],
        "L1_attn_w1": _L1_attn_in["w1"],
        "L1_attn_b1": _L1_attn_in["b1"],
        "L1_attn_w2": _L1_attn_in["w2"],
        "L1_attn_b2": _L1_attn_in["b2"],
        "L1_attn_g1": _L1_attn_in["g1"],
        "L1_attn_beta1": _L1_attn_in["beta1"],
        "L1_attn_g2": _L1_attn_in["g2"],
        "L1_attn_beta2": _L1_attn_in["beta2"],
        "L1_ffn_gate_w": _L1_ffn_in["gate_w"],
        "L1_ffn_gate_b": _L1_ffn_in["gate_b"],
        "L1_ffn_weight1": _L1_ffn_in["weight1"],
        "L1_ffn_weight2": _L1_ffn_in["weight2"],
    }

def reference(x, L0_conv_offset_w, L0_conv_offset_b, L0_conv_dcn_w, L1_attn_rx_theta, L1_attn_ry_theta, L1_attn_w_comb, L1_attn_b_comb, L1_attn_w1, L1_attn_b1, L1_attn_w2, L1_attn_b2, L1_attn_g1, L1_attn_beta1, L1_attn_g2, L1_attn_beta2, L1_ffn_gate_w, L1_ffn_gate_b, L1_ffn_weight1, L1_ffn_weight2):
    import jax
    import jax.numpy as jnp
    def _L0_conv_ref(x, offset_w, offset_b, dcn_w):
        import jax, jax.numpy as jnp
        import numpy as np
        from jax import lax
        IN_C = 128
        OUT_C = 128
        K = 3
        STRIDE = 1
        PAD = 1
        N, H, W = (4, 64, 64)

        def _dcn_forward(x, offset_w, offset_b, dcn_w):
            n, in_c, h, w = x.shape
            out_c, _, kh, kw = dcn_w.shape
            kk = kh * kw
            f32 = x.dtype
            om = lax.conv_general_dilated(x, offset_w, (STRIDE, STRIDE), [(PAD, PAD), (PAD, PAD)], dimension_numbers=('NCHW', 'OIHW', 'NCHW')) + offset_b[None, :, None, None]
            off_y = jnp.transpose(om[:, 0:2 * kk:2], (0, 2, 3, 1))
            off_x = jnp.transpose(om[:, 1:2 * kk:2], (0, 2, 3, 1))
            mask = jax.nn.sigmoid(jnp.transpose(om[:, 2 * kk:], (0, 2, 3, 1)))
            out_h = (h + 2 * PAD - (kh - 1)) // STRIDE
            out_w = (w + 2 * PAD - (kw - 1)) // STRIDE
            pad_x = jnp.pad(x, ((0, 0), (0, 0), (PAD, PAD + 1), (PAD, PAD + 1)))
            pad_x = jnp.transpose(pad_x, (0, 2, 3, 1))
            base_y = (jnp.arange(out_h, dtype=f32) * STRIDE + PAD)[None, :, None, None]
            base_x = (jnp.arange(out_w, dtype=f32) * STRIDE + PAD)[None, None, :, None]
            half = (kw - 1) // 2
            inner_y = jnp.repeat(jnp.arange(kh, dtype=f32) - half, kw)
            inner_x = jnp.tile(jnp.arange(kw, dtype=f32) - half, kh)
            pos_y = jnp.clip(base_y + inner_y + off_y, 0.0, h + 2 * PAD - 1.0)
            pos_x = jnp.clip(base_x + inner_x + off_x, 0.0, w + 2 * PAD - 1.0)
            y1 = jnp.floor(pos_y)
            x1 = jnp.floor(pos_x)
            y1i = y1.astype(jnp.int32)
            x1i = x1.astype(jnp.int32)
            y2i = y1i + 1
            x2i = x1i + 1
            n_idx = jnp.arange(n)[:, None, None, None]
            v1 = pad_x[n_idx, y1i, x1i]
            v2 = pad_x[n_idx, y1i, x2i]
            v3 = pad_x[n_idx, y2i, x1i]
            v4 = pad_x[n_idx, y2i, x2i]
            lh = (pos_y - y1)[..., None]
            lw = (pos_x - x1)[..., None]
            hh = 1.0 - lh
            hw = 1.0 - lw
            value = (hh * hw * v1 + hh * lw * v2 + lh * hw * v3 + lh * lw * v4) * mask[..., None]
            out = jnp.einsum('nhwkc,ock->nohw', value, dcn_w.reshape(out_c, in_c, kk))
            return out
        return _dcn_forward(x, offset_w, offset_b, dcn_w)

    def _L1_attn_ref(x, rx_theta, ry_theta, w_comb, b_comb, w1, b1, w2, b2, g1, beta1, g2, beta2):
        import jax, jax.numpy as jnp
        import numpy as np
        B, S, H, D = (8, 1024, 16, 8)
        E, FFN = (H * D, 512)
        NQ_FFN = 8
        EPS = 1e-05

        def _qz_ring(phi):
            c = jnp.cos(phi)
            P = jnp.cumprod(c, axis=-1)
            z0 = jnp.prod(c[..., 1:], axis=-1, keepdims=True)
            return jnp.concatenate([z0, P[..., 1:]], axis=-1)

        def _ln(v, g, b):
            mu = jnp.mean(v, axis=-1, keepdims=True)
            var = jnp.mean((v - mu) ** 2, axis=-1, keepdims=True)
            return (v - mu) * jax.lax.rsqrt(var + EPS) * g + b
        Bs, Ss, Es = x.shape
        heads = x.reshape(Bs, Ss, H, D)
        qkv = _qz_ring(heads + rx_theta)
        q = jnp.transpose(qkv, (0, 2, 1, 3))
        scores = jnp.einsum('bhsd,bhtd->bhst', q, q) / np.sqrt(D)
        attn = jax.nn.softmax(scores, axis=-1)
        ctx = jnp.einsum('bhst,bhtd->bhsd', attn, q)
        ctx = jnp.transpose(ctx, (0, 2, 1, 3)).reshape(Bs, Ss, Es)
        attn_out = ctx @ w_comb.T + b_comb
        x1 = _ln(x + attn_out, g1, beta1)
        zf = jnp.cos(x1[..., :NQ_FFN]) * jnp.cos(ry_theta)
        h = jax.nn.relu(zf @ w1.T + b1)
        ffn_out = h @ w2.T + b2
        return _ln(x1 + ffn_out, g2, beta2)

    def _L1_ffn_ref(x, gate_w, gate_b, weight1, weight2):
        import jax, jax.numpy as jnp
        import numpy as np
        B, S, D, E, H, O, K = (512, 2048, 128, 64, 512, 128, 8)
        Bn, Sn, Dn = x.shape
        logits = jnp.einsum('bsd,ed->bse', x, gate_w) + gate_b
        probs = jax.nn.softmax(logits, axis=1)
        vals, idx = jax.lax.top_k(probs.transpose(0, 2, 1), K)
        topv = vals.transpose(0, 2, 1)
        topi = idx.transpose(0, 2, 1)
        flat_idx = topi.reshape(Bn, K * E)
        gathered = jnp.take_along_axis(x, flat_idx[:, :, None], axis=1)
        gathered = gathered.reshape(Bn, K, E, Dn)
        pooled = jnp.einsum('bked,bke->bed', gathered, topv)
        ones = jnp.ones((E, Bn, 1), dtype=x.dtype)
        h = jnp.concatenate([pooled.transpose(1, 0, 2), ones], axis=-1)
        h = jax.nn.gelu(jnp.einsum('ebd,edh->ebh', h, weight1), approximate=False)
        h = jnp.concatenate([h, ones], axis=-1)
        out = jnp.einsum('ebh,eho->ebo', h, weight2)
        out = out.transpose(1, 0, 2)
        weighted = jnp.einsum('beo,bke->bkeo', out, topv).reshape(Bn, K * E, O)
        outputs = jnp.zeros((Bn, Sn, O), dtype=x.dtype)
        outputs = outputs.at[jnp.arange(Bn)[:, None], flat_idx].add(weighted)
        return outputs

    def _gn(v, G=32, eps=1e-5):
        B_, C_, H_, W_ = v.shape
        g = v.reshape(B_, G, C_ // G, H_, W_)
        m = jnp.mean(g, axis=(2, 3, 4), keepdims=True)
        s = jnp.var(g, axis=(2, 3, 4), keepdims=True)
        return ((g - m) / jnp.sqrt(s + eps)).reshape(v.shape)

    def _ln_c(v, eps=1e-6):
        m = jnp.mean(v, axis=1, keepdims=True)
        s = jnp.var(v, axis=1, keepdims=True)
        return (v - m) / jnp.sqrt(s + eps)

    def _ln_t(v, eps=1e-5):
        m = jnp.mean(v, axis=-1, keepdims=True)
        s = jnp.var(v, axis=-1, keepdims=True)
        return (v - m) / jnp.sqrt(s + eps)

    def _to_tokens(v):
        B_, C_, H_, W_ = v.shape
        return v.reshape(B_, C_, H_ * W_).transpose(0, 2, 1)
    def _from_tokens(t, like):
        B_, C_, H_, W_ = like.shape
        return t.transpose(0, 2, 1).reshape(B_, C_, H_, W_)

    x = x + _L0_conv_ref(_gn(x), L0_conv_offset_w, L0_conv_offset_b, L0_conv_dcn_w)
    t = _to_tokens(x)
    t = t + _L1_attn_ref(_ln_t(t), L1_attn_rx_theta, L1_attn_ry_theta, L1_attn_w_comb, L1_attn_b_comb, L1_attn_w1, L1_attn_b1, L1_attn_w2, L1_attn_b2, L1_attn_g1, L1_attn_beta1, L1_attn_g2, L1_attn_beta2)
    t = t + _L1_ffn_ref(_ln_t(t), L1_ffn_gate_w, L1_ffn_gate_b, L1_ffn_weight1, L1_ffn_weight2)
    x = _from_tokens(t, x)
    return x


_drawn_inputs = setup_inputs


def setup_inputs(seed=0):
    import zlib

    import numpy as np

    out = dict(_drawn_inputs(seed))
    spreads = {'L0_conv_offset_b': (0.0, 0.1),
     'L1_attn_b_comb': (0.0, 0.1),
     'L1_attn_b1': (0.0, 0.1),
     'L1_attn_b2': (0.0, 0.1),
     'L1_attn_g1': (1.0, 0.2),
     'L1_attn_beta1': (0.0, 0.1),
     'L1_attn_g2': (1.0, 0.2),
     'L1_attn_beta2': (0.0, 0.1),
     'L1_ffn_gate_b': (0.0, 0.1)}
    factors = {'L1_attn_rx_theta': 3.323,
     'L1_ffn_gate_w': 8.0,
     'L1_ffn_weight1': 8.0,
     'L1_ffn_weight2': 8.0}
    for name, (base, spread) in spreads.items():
        noise = np.random.default_rng([zlib.crc32(name.encode()), seed]).standard_normal(out[name].shape)
        drawn = base * np.exp(spread * noise) if base else spread * noise
        out[name] = jnp.asarray(drawn.astype(out[name].dtype))
    for name, factor in factors.items():
        out[name] = (out[name] * factor).astype(out[name].dtype)
    return out
```

```python
from contextlib import ExitStack

import numpy as np
import concourse.bass as bass
from concourse import mybir

F32 = mybir.dt.float32
F16 = mybir.dt.float16
I32 = mybir.dt.int32
ALU = mybir.AluOpType
ACT = mybir.ActivationFunctionType
AX = mybir.AxisListType.X

P = 128
IMAGES, CH, SIDE = 4, 128, 64
TOK = SIDE * SIDE
TILES = TOK // P
TAPS = 9
PADW = SIDE + 3
NPAD = 36
PADPIX = NPAD * P
MARGIN = 128
TROWS = MARGIN + PADPIX
CORNERS = (0, 1, PADW, PADW + 1)
HEADS, HD = 16, 8
QUADS = HEADS // 4
CHUNK = 512
UNITS = TOK // CHUNK
FFN = 512
NEXP, TOPK = 64, 8
PAIRS = IMAGES * TILES // 2
QPAIRS = UNITS // 2
MAGIC = 12582912.0
TWO_PI_HI, TWO_PI_LO = 6.28125, 0.0019353071795864769
RSQRT_SEED = 1597463007.0
SIN_HALF = [(-1) ** k / (2.0 ** (2 * k + 1)) / float(np.prod(np.arange(1, 2 * k + 2, dtype=np.float64))) for k in range(8)]


class Steps:

    def __init__(self, eng, sem, base=0):
        self.eng, self.sem, self.base, self.n = eng, sem, base, 0

    def inc(self, ins):
        self.n += 1
        return ins.then_inc(self.sem, 1)

    def wait(self, eng=None, back=0):
        (eng or self.eng).wait_ge(self.sem, self.base + (self.n - back))

    def link(self, ins):
        self.inc(ins)
        self.wait()


def bcast(ap2, n):
    return ap2.rearrange("p (a o) -> p a o", o=1).to_broadcast([ap2.shape[0], ap2.shape[1], n])


def layer_norm(nc, st, out, x, tmp, stat, n, w, eps, gain=None, shift=None):
    v = nc.vector
    s, m, y, b = stat[:, 0, 0:n], stat[:, 1, 0:n], stat[:, 2, 0:n], stat[:, 3, 0:n]
    st.link(v.tensor_reduce(s, x, AX, ALU.add))
    st.link(v.tensor_scalar(m, s, 1.0 / w, None, ALU.mult))
    st.link(v.tensor_tensor(out, x, bcast(m, w), ALU.subtract))
    st.link(v.tensor_tensor(tmp, out, out, ALU.mult))
    st.link(v.tensor_reduce(s, tmp, AX, ALU.add))
    st.link(v.tensor_scalar(s, s, 1.0 / w, eps, ALU.mult, ALU.add))
    rsqrt(nc, st, y, s, m, b)
    st.link(v.tensor_tensor(out, out, bcast(y, w), ALU.mult))
    if gain is not None:
        p = x.shape[0]
        g = gain.rearrange("p (o w) -> p o w", o=1).to_broadcast([p, n, w])
        h = shift.rearrange("p (o w) -> p o w", o=1).to_broadcast([p, n, w])
        st.link(v.tensor_tensor(out, out, g, ALU.mult))
        st.link(v.tensor_tensor(out, out, h, ALU.add))


def rsqrt(nc, st, y, x, a, b):
    v = nc.vector
    st.link(v.tensor_scalar(a.bitcast(I32), x.bitcast(I32), 1, None, ALU.logical_shift_right))
    st.link(v.tensor_scalar(y.bitcast(I32), a.bitcast(I32), -1.0, RSQRT_SEED, ALU.mult, ALU.add))
    for _ in range(3):
        st.link(v.scalar_tensor_tensor(out=a, in0=y, scalar=-0.5, in1=y, op0=ALU.mult, op1=ALU.mult))
        st.link(v.tensor_tensor(b, a, x, ALU.mult))
        st.link(v.scalar_tensor_tensor(out=y, in0=b, scalar=1.5, in1=y, op0=ALU.add, op1=ALU.mult))


def cosine(nc, st, x, k, z, p):
    v = nc.vector
    st.link(v.tensor_scalar(k, x, 1.0 / (2 * np.pi), MAGIC, ALU.mult, ALU.add))
    st.link(v.tensor_scalar(k, k, MAGIC, None, ALU.subtract))
    st.link(v.scalar_tensor_tensor(out=x, in0=k, scalar=-TWO_PI_HI, in1=x, op0=ALU.mult, op1=ALU.add))
    st.link(v.scalar_tensor_tensor(out=x, in0=k, scalar=-TWO_PI_LO, in1=x, op0=ALU.mult, op1=ALU.add))
    st.link(v.tensor_tensor(z, x, x, ALU.mult))
    st.link(v.tensor_scalar(p, z, SIN_HALF[-1], SIN_HALF[-2], ALU.mult, ALU.add))
    st.link(v.tensor_tensor(p, p, z, ALU.mult))
    for c in SIN_HALF[-3:0:-1]:
        st.link(v.scalar_tensor_tensor(out=p, in0=p, scalar=c, in1=z, op0=ALU.add, op1=ALU.mult))
    st.link(v.scalar_tensor_tensor(out=p, in0=p, scalar=SIN_HALF[0], in1=x, op0=ALU.add, op1=ALU.mult))
    st.link(v.scalar_tensor_tensor(out=z, in0=p, scalar=-2.0, in1=p, op0=ALU.mult, op1=ALU.mult))
    st.link(v.tensor_scalar(x, z, 1.0, None, ALU.add))


def stage_offsets(nc, d, r, stack):
    sb = lambda n, s, t=F32: stack.enter_context(nc.sbuf_tensor(n, s, t))
    sem = lambda n: stack.enter_context(nc.semaphore(n))
    x_ch = sb("x_ch", [P, TOK])
    xpad = sb("xpad", [P, PADPIX])
    zero = sb("zero", [P, 4 * P])
    zeroed, edges = sem("zeroed"), sem("edges")
    pix = sb("pix", [P, NPAD, P])
    om = sb("om", [P, TILES, 27])
    pos = [sb(f"pos{i}", [P, TILES, TAPS]) for i in range(6)]
    offw, offb, base, gmat = sb("offw", [P, TAPS, 27]), sb("offb", [P, 27]), sb("base", [P, 2, TILES, TAPS]), sb("gmat", [P, P])
    bn, agg, gs = sb("bn", [P, 8, 6]), sb("agg", [P, 2]), sb("gs", [P, 8])
    ps_om = stack.enter_context(nc.psum_tensor("ps_om", [P, 2, 512], F32))
    ps_t = stack.enter_context(nc.psum_tensor("ps_t", [P, 2, 512], F32))
    ps_g = stack.enter_context(nc.psum_tensor("ps_g", [P, 512], F32))
    consts, x_loaded, x_read = sem("c1_consts"), sem("x_loaded"), sem("x_read")
    dv, stat_ready, group_ready, padded = sem("c1_dve"), sem("stat_ready"), sem("group_ready"), sem("padded")
    om_full, om_read, tr_full, tr_free = sem("om_full"), sem("om_read"), sem("tr_full"), sem("tr_free")
    tables, om_ready, sig, summed = sem("tables"), sem("om_ready"), sem("sig"), sem("summed")
    interior = xpad[:, 0:PADW * (SIDE + 2)].rearrange("p (y x) -> p y x", x=PADW)
    NG = NPAD // 4
    DVE_STEPS = 36

    block = stack.enter_context(nc.Block())

    @block.sync
    def _(sp):
        for dst, src in ((offw, d.offw), (offb, d.offb), (base, d.base), (gmat, d.gmat)):
            sp.dma_start(dst[:], src).then_inc(consts, 16)
        sp.wait_ge(zeroed, 1)
        for i in range(IMAGES):
            for row in (i * TROWS, (i + 1) * TROWS - P):
                sp.dma_start(d.table[row:row + P, :], zero[:]).then_inc(edges, 16)
        with sp.Fori(0, IMAGES) as b:
            sp.wait_ge(edges, 2 * IMAGES * 16)
            sp.wait_ge(x_read, b)
            sp.dma_start(x_ch[:], d.x[bass.ds(b, 1)].rearrange("o c n -> (o c) n")).then_inc(x_loaded, 16)
            sp.wait_ge(tr_free, (b + 1) * NG)
            for c, off in enumerate(CORNERS):
                dst = d.table[bass.ds(b * TROWS + (MARGIN - off), PADPIX), c * P:(c + 1) * P]
                sp.dma_start(dst.rearrange("(i p) c -> p i c", p=P), pix[:]).then_inc(tables, 16)
        sp.wait_ge(tables, IMAGES * 64)

    @block.vector
    def _(dve):
        v = nc.vector
        dve.wait_ge(consts, 64)
        v.memset(zero[:], 0.0).then_inc(zeroed, 1)
        v.memset(xpad[:], 0.0).then_inc(dv, 1)
        dve.wait_ge(dv, 1)
        with dve.Fori(0, IMAGES) as b:
            st = Steps(dve, dv, b * DVE_STEPS + 1)
            dve.wait_ge(x_loaded, (b + 1) * 16)
            for j in range(8):
                last = v.bn_stats(bn[:, j, :], x_ch[:, j * 512:(j + 1) * 512])
            st.link(last)
            dve.sem_inc(summed, 1)
            st.link(v.bn_aggr(agg[:], bn[:].rearrange("p a b -> p (a b)")))
            v.tensor_copy(gs[:, 0:1], agg[:, 0:1]).then_inc(stat_ready, 1)
            dve.wait_ge(group_ready, 2 * b + 1)
            st.link(v.tensor_copy(gs[:, 1:2], ps_g[:, 0:1]))
            st.link(v.tensor_tensor(gs[:, 2:3], agg[:, 0:1], gs[:, 1:2], ALU.subtract))
            st.link(v.tensor_tensor(gs[:, 2:3], gs[:, 2:3], gs[:, 2:3], ALU.mult))
            v.tensor_tensor(gs[:, 3:4], gs[:, 2:3], agg[:, 1:2], ALU.add).then_inc(stat_ready, 1)
            dve.wait_ge(group_ready, 2 * b + 2)
            st.link(v.tensor_scalar(gs[:, 4:5], ps_g[:, 1:2], 1e-5, None, ALU.add))
            rsqrt(nc, st, gs[:, 5:6], gs[:, 4:5], gs[:, 6:7], gs[:, 7:8])
            dve.wait_ge(tr_full, b * NG)
            v.tensor_scalar(interior[:, 1:SIDE + 1, 1:SIDE + 1], x_ch[:].rearrange("p (y x) -> p y x", x=SIDE),
                            gs[:, 1:2], gs[:, 5:6], ALU.subtract, ALU.mult).then_inc(padded, 1)
            dve.wait_ge(padded, b + 1)
            dve.sem_inc(x_read, 1)
            obias = offb[:].rearrange("p (o c) -> p o c", o=1).to_broadcast([P, 16, 27])
            for half in range(2):
                dve.wait_ge(om_full, 2 * b + half + 1)
                ins = v.tensor_tensor(om[:, half * 16:half * 16 + 16, :],
                                      ps_om[:, half, 0:432].rearrange("p (t c) -> p t c", c=27), obias, ALU.add)
                ins.then_inc(om_read, 1)
            dve.wait_ge(om_read, 2 * b + 2)
            dve.sem_inc(om_ready, 1)
            py, px, fy, fx, t0, mask = [q[:] for q in pos]
            for q, axis in ((py, 0), (px, 1)):
                st.link(v.tensor_tensor(q, om[:, :, axis:18:2], base[:, axis], ALU.add))
                st.link(v.tensor_scalar(q, q, 0.0, SIDE + 1.0, ALU.max, ALU.min))
            for q, f in ((py, fy), (px, fx)):
                st.link(v.tensor_scalar(f, q, MAGIC, MAGIC, ALU.add, ALU.subtract))
                st.link(v.tensor_tensor(t0, f, q, ALU.is_gt))
                st.link(v.tensor_tensor(f, f, t0, ALU.subtract))
                st.link(v.tensor_tensor(q, q, f, ALU.subtract))
            flat = lambda q: q.rearrange("p t k -> p (t k)")
            st.link(v.scalar_tensor_tensor(out=t0, in0=fy, scalar=float(PADW), in1=fx, op0=ALU.mult, op1=ALU.add))
            idx = r.idx[:, bass.ds(b * (TILES * TAPS), TILES * TAPS)]
            st.link(v.tensor_scalar(idx, flat(t0), r.image_row[:, bass.ds(b, 1)], None, ALU.add))
            dve.wait_ge(sig, b + 1)
            wt = r.wts[:, bass.ds(b * TILES, TILES)]
            st.link(v.tensor_scalar(fy, py, -1.0, 1.0, ALU.mult, ALU.add))
            st.link(v.tensor_tensor(fy, fy, mask, ALU.mult))
            st.link(v.tensor_tensor(py, py, mask, ALU.mult))
            v.tensor_tensor(wt[:, :, :, 1], fy, px, ALU.mult)
            v.tensor_tensor(wt[:, :, :, 3], py, px, ALU.mult)
            st.link(v.tensor_scalar(fx, px, -1.0, 1.0, ALU.mult, ALU.add))
            v.tensor_tensor(wt[:, :, :, 0], fy, fx, ALU.mult)
            st.link(v.tensor_tensor(wt[:, :, :, 2], py, fx, ALU.mult))
            DVE = st.n
        assert DVE == DVE_STEPS, DVE

    @block.scalar
    def _(act):
        with act.Fori(0, IMAGES) as b:
            for g in range(NG):
                act.wait_ge(tr_full, b * NG + g + 1)
                if g == 0:
                    act.wait_ge(tables, b * 64)
                nc.scalar.copy(pix[:, 4 * g:4 * g + 4, :].rearrange("p a c -> p (a c)"), ps_t[:, g % 2, :]).then_inc(tr_free, 1)
            act.wait_ge(om_ready, b + 1)
            nc.scalar.activation(pos[5][:], om[:, :, 18:27], ACT.Sigmoid).then_inc(sig, 1)

    @block.tensor
    def _(pe):
        pe.wait_ge(consts, 64)
        with pe.Fori(0, IMAGES) as b:
            for k, col in ((0, 0), (1, 3)):
                pe.wait_ge(stat_ready, 2 * b + k + 1)
                nc.tensor.matmul(ps_g[:, k:k + 1], gmat[:], gs[:, col:col + 1], start=True, stop=True).then_inc(group_ready, 1)
            pe.wait_ge(padded, b + 1)
            for half in range(2):
                pe.wait_ge(om_read, 2 * b)
                for i in range(half * 16, half * 16 + 16):
                    for k in range(TAPS):
                        ky, kx = divmod(k, 3)
                        for row in range(2):
                            px = interior[:, 2 * i + row + ky, kx:kx + SIDE]
                            last = nc.tensor.matmul(ps_om[row * SIDE:(row + 1) * SIDE, half, (i % 16) * 27:(i % 16) * 27 + 27],
                                                    px, offw[:, k, :], start=(k == 0), stop=(k == TAPS - 1))
                last.then_inc(om_full, 1)
            for g in range(NG):
                if g >= 2:
                    pe.wait_ge(tr_free, b * NG + g - 1)
                elif g == 0:
                    pe.wait_ge(tr_free, b * NG)
                for j in range(4):
                    i = 4 * g + j
                    last = nc.tensor.transpose(ps_t[:, g % 2, j * P:(j + 1) * P], xpad[:, i * P:(i + 1) * P], r.ident[:])
                last.then_inc(tr_full, 1)


def token_pair(t, n):
    return t[bass.ds(n * 256, 256), :].rearrange("(t p) c -> p t c", p=P)


class ConvStep:

    def __init__(self, nc, d, r, stack, misc):
        sb = lambda n, s, t=F32: stack.enter_context(nc.sbuf_tensor(n, s, t))
        sem = lambda n: stack.enter_context(nc.semaphore(n))
        self.nc, self.d, self.r, self.misc = nc, d, r, misc
        self.idx_st = [sb(f"idx_st{s}", [P, TAPS], I32) for s in range(2)]
        self.w_st = [sb(f"w_st{s}", [P, TAPS, 4]) for s in range(2)]
        self.corners = [sb(f"corners{s}", [P, TAPS, 512]) for s in range(2)]
        self.val = [sb(f"val{s}", [P, TAPS, P]) for s in range(2)]
        self.val_t = sb("val_t", [P, TAPS * P])
        self.xt = sb("xt", [P, 2, P])
        self.t1 = sb("t1_out", [P, 2, P])
        self.xn, self.ph, self.tmp, self.tmp2, self.tmp3 = (sb(n, [P, 2, P]) for n in ("xn", "ph", "ctmp", "ctmp2", "ctmp3"))
        self.cum = sb("cum", [P, 2 * HEADS, 2])
        self.q = sb("q_out", [P, 2, P])
        self.stat = sb("cstat", [P, 4, 2])
        self.dv, self.idx_ready, self.w_copied = sem("conv_dve"), sem("idx_ready"), sem("w_copied")
        self.gathered = [sem(f"gathered{s}") for s in range(2)]
        self.gathering, self.val_ready, self.x_in, self.t1_ready, self.q_ready, self.stored = (
            sem(n) for n in ("gathering", "val_ready", "x_in", "t1_ready", "q_ready", "conv_stored"))

    def load_sp(self, sp, n):
        sp.wait_ge(self.t1_ready, n)
        sp.dma_start(self.xt[:], token_pair(self.d.x_tok, n)).then_inc(self.x_in, 16)

    def store_sp(self, sp, n):
        sp.wait_ge(self.t1_ready, n + 1)
        sp.dma_start(token_pair(self.d.t1, n), self.t1[:]).then_inc(self.stored, 16)
        sp.wait_ge(self.q_ready, n + 1)
        for t in range(2):
            dst = self.d.q[:, bass.ds(n * 256 + t * P, P), :].rearrange("g p c -> p g c")
            sp.dma_start(dst, self.q[:, t, :].rearrange("p (g c) -> p g c", g=QUADS)).then_inc(self.stored, 16)

    def pool(self, pool, n):
        for s in range(2):
            pool.wait_ge(self.idx_ready, 2 * n + s + 1)
            pool.wait_ge(self.val_ready, 2 * n + s + 1)
            pool.sem_inc(self.gathering, 1)
            for k in range(TAPS):
                pool.indirect_dma_start(self.corners[s][:, k, :], None, self.d.table,
                                        bass.IndirectOffsetOnAxis(self.idx_st[s][:, k:k + 1], 0)).then_inc(self.gathered[s], 16)

    STEPS = 53

    def stage_dve(self, dve, n, s):
        v, r = self.nc.vector, self.r
        v.tensor_copy(self.w_st[s][:].rearrange("p k c -> p (k c)"),
                      r.wts[:, bass.ds(2 * n + s, 1)].rearrange("p o k c -> p (o k c)")).then_inc(self.w_copied, 1)
        v.tensor_copy(self.idx_st[s][:], r.idx[:, bass.ds((2 * n + s) * TAPS, TAPS)]).then_inc(self.idx_ready, 1)

    def sample_dve(self, dve, n, s, st):
        v = self.nc.vector
        dve.wait_ge(self.gathered[s], (n + 1) * (16 * TAPS))
        dve.wait_ge(self.w_copied, 2 * n + s + 1)
        g, val, w = self.corners[s], self.val[s], self.w_st[s]
        for c in range(4):
            for k in range(TAPS):
                src, wt = g[:, k, c * P:(c + 1) * P], w[:, k, c:c + 1]
                if c == 0:
                    last = v.tensor_scalar(val[:, k, :], src, wt, None, ALU.mult)
                else:
                    last = v.scalar_tensor_tensor(out=val[:, k, :], in0=src, scalar=wt, in1=val[:, k, :],
                                                  op0=ALU.mult, op1=ALU.add)
            if c < 3:
                st.link(last)
        last.then_inc(self.val_ready, 1)
        dve.wait_ge(self.val_ready, 2 * n + s + 3)
        self.stage_dve(dve, (n + 1) % PAIRS, s)

    def product_dve(self, dve, n, s):
        v, m = self.nc.vector, self.misc
        for g0, g1 in self.GROUPS:
            m.dve_take(dve)
            m.dve_give(v.tensor_copy(self.val_t[:, g0 * P:g1 * P], m.bank[:, 0:(g1 - g0) * P]))
        m.dve_take(dve)
        if s == 0:
            dve.wait_ge(self.x_in, (n + 1) * 16)
            dve.wait_ge(self.stored, n * 48)
        m.dve_give(v.tensor_tensor(self.t1[:, s, :], m.bank[:, 0:P], self.xt[:, s, :], ALU.add))

    def ring_dve(self, dve, n, st):
        nc, r, m = self.nc, self.r, self.misc
        v = nc.vector
        m.dve_wait_given(dve)
        dve.sem_inc(self.t1_ready, 1)
        layer_norm(nc, st, self.xn[:], self.t1[:], self.tmp[:], self.stat, 2, P, 1e-5)
        theta = r.theta[:].rearrange("p (o w) -> p o w", o=1).to_broadcast([P, 2, P])
        st.link(v.tensor_tensor(self.ph[:], self.xn[:], theta, ALU.add))
        cosine(nc, st, self.ph[:], self.tmp[:], self.tmp2[:], self.tmp3[:])
        c = self.ph[:].rearrange("p t (h d) -> p (t h) d", d=HD)
        q = self.q[:].rearrange("p t (h d) -> p (t h) d", d=HD)
        st.inc(v.tensor_tensor(q[:, :, 1], c[:, :, 0], c[:, :, 1], ALU.mult))
        st.link(v.tensor_tensor(self.cum[:, :, 0], c[:, :, 1], c[:, :, 2], ALU.mult))
        for j in range(2, HD):
            st.inc(v.tensor_tensor(q[:, :, j], q[:, :, j - 1], c[:, :, j], ALU.mult))
            if j + 1 < HD:
                dst = q[:, :, 0] if j + 1 == HD - 1 else self.cum[:, :, (j + 1) % 2]
                st.inc(v.tensor_tensor(dst, self.cum[:, :, j % 2], c[:, :, j + 1], ALU.mult))
            st.wait()
        dve.sem_inc(self.q_ready, 1)

    GROUPS = ((0, 4), (4, 8), (8, 9))

    def transposes_pe(self, pe, n, s, g):
        m = self.misc
        if g == 0:
            pe.wait_ge(self.val_ready, 2 * n + s + 3)
        g0, g1 = self.GROUPS[g]
        m.pe_take(pe)
        for k in range(g0, g1):
            last = self.nc.tensor.transpose(m.bank[:, (k - g0) * P:(k - g0 + 1) * P], self.val[s][:, k, :], self.r.ident[:])
        m.pe_give(last)

    def product_pe(self, pe, part):
        m = self.misc
        if part == 0:
            m.pe_take(pe)
        for k in range(3 * part, 3 * part + 3):
            last = self.nc.tensor.matmul(m.bank[:, 0:P], self.val_t[:, k * P:(k + 1) * P], self.r.dcnw[:, k, :],
                                         start=(k == 0), stop=(k == TAPS - 1))
        if part == 2:
            m.pe_give(last)

    def items_pe(self, pe, n, s):
        return ([lambda g=g: self.transposes_pe(pe, n, s, g) for g in range(3)]
                + [lambda i=i: self.product_pe(pe, i) for i in range(3)])


class Misc:

    def __init__(self, bank, full, free):
        self.bank, self.full, self.free = bank, full, free
        self.base, self.p, self.d = 0, 0, 0

    def start(self, base):
        self.base, self.p, self.d = base, 0, 0

    def pe_take(self, pe):
        pe.wait_ge(self.free, self.base + (self.p + 1))

    def pe_give(self, ins):
        self.p += 1
        ins.then_inc(self.full, 1)

    def dve_take(self, dve):
        dve.wait_ge(self.full, self.base + (self.d + 1))

    def dve_give(self, ins):
        self.d += 1
        ins.then_inc(self.free, 1)

    def dve_wait_given(self, dve):
        dve.wait_ge(self.free, self.base + (self.d + 1))


class AttnStep:

    SC, NE = 3, 8
    STEPS = 2 * TILES * 2
    UNIT = TILES
    PV_START = NE // 2

    def __init__(self, nc, d, r, stack, misc):
        sb = lambda n, s, t=F32: stack.enter_context(nc.sbuf_tensor(n, s, t))
        sem = lambda n: stack.enter_context(nc.semaphore(n))
        self.nc, self.d, self.r, self.misc = nc, d, r, misc
        self.qn = sb("qn", [P, TILES, 4 * HD])
        self.wa, self.wb = (sb(n, [P, 8, 4, 4, HD], F16) for n in ("wa", "wb"))
        self.a_next, self.a = (sb(n, [P, TOK], F16) for n in ("a_next", "a_cur"))
        self.b = sb("b_two_quads", [P, 2 * TOK], F16)
        self.v_next, self.v = (sb(n, [P, TILES, 4, HD + 1]) for n in ("v_next", "v_cur"))
        self.bst = [sb(f"b_unit{s}", [P, 4, CHUNK], F16) for s in range(2)]
        self.e = [sb(f"e{i}", [P, 2, CHUNK]) for i in range(self.NE)]
        self.acc_sb, self.rs = sb("acc_sb", [P, CHUNK]), sb("rs", [P, 16])
        self.ctx_t = [sb(f"ctx_t{s}", [P, 4, 4 * HD]) for s in range(2)]
        self.sc = [stack.enter_context(nc.psum_tensor(f"sc{i}", [P, 2, CHUNK], F32)) for i in range(self.SC)]
        self.acc = stack.enter_context(nc.psum_tensor("acc", [P, CHUNK], F32))
        (self.q_in, self.staged, self.a_switched, self.v_switched, self.units_ready, self.sc_ready, self.exp_done,
         self.pv_done, self.acc_read, self.dv_stage, self.dv_finish, self.w_ready, self.ctx_ready, self.init) = (sem(n) for n in (
             "q_in", "q_staged", "a_switched", "v_switched", "units_ready", "sc_ready", "exp_done",
             "pv_done", "acc_read", "stage_dve", "finish_dve", "w_ready", "ctx_ready", "attn_init"))
        self.ctx_stored = [sem(f"ctx_stored{s}") for s in range(2)]

    def init_dve(self, dve):
        v = self.nc.vector
        v.memset(self.acc[:], 1.0).then_inc(self.init, 1)
        v.memset(self.v_next[:], 1.0).then_inc(self.init, 1)
        for s in range(2):
            v.memset(self.bst[s][:], 0.0).then_inc(self.init, 1)
        dve.wait_ge(self.init, 4)

    def load_q(self, sp, qd):
        sp.wait_ge(self.staged, 4 * qd)
        src = self.d.q[bass.ds(qd % QUADS, 1), bass.ds((qd // QUADS) * TOK, TOK), :].rearrange("g (t p) c -> p (g t) c", p=P)
        sp.dma_start(self.qn[:], src).then_inc(self.q_in, 16)

    def stage_dve(self, dve, qd, p):
        v, m = self.nc.vector, self.misc
        st = Steps(dve, self.dv_stage, (4 * qd + p) * 2)
        dve.wait_ge(self.a_switched, qd)
        dve.wait_ge(self.v_switched, qd)
        dve.wait_ge(self.q_in, (qd + 1) * 16)
        q = self.qn[:, bass.ds(p * 8, 8), :].rearrange("p t (h d) -> p (t h) d", d=HD)
        wa = self.wa[:].rearrange("p t h v d -> p (t h) v d")
        wb = self.wb[:].rearrange("p t h v d -> p (t h) v d")
        vn = self.v_next[:, bass.ds(p * 8, 8)].rearrange("p t h e -> p (t h) e")
        v.tensor_copy(vn[:, :, 0:HD], q)
        st.link(v.tensor_copy(wa[:, :, 0, :], q))
        v.tensor_tensor(wa[:, :, 1, :], q, wa[:, :, 0, :], ALU.subtract).then_inc(self.staged, 1)
        dve.wait_ge(self.staged, 4 * qd + p + 1)
        v.tensor_copy(wa[:, :, 2:4, :], wa[:, :, 0:2, :])
        v.tensor_copy(wb[:, :, 0:2, :], wa[:, :, 0:2, :])
        v.tensor_copy(wb[:, :, 2, :], wa[:, :, 1, :])
        st.link(v.tensor_copy(wb[:, :, 3, :], wa[:, :, 0, :]))
        dve.sem_inc(self.w_ready, 1)
        m.dve_take(dve)
        m.dve_give(v.tensor_copy(self.a_next[:, bass.ds(p * 1024, 1024)], m.bank[:].bitcast(F16)))
        m.dve_take(dve)
        m.dve_give(v.tensor_copy(self.b[:, bass.ds((qd % 2) * TOK + p * 1024, 1024)], m.bank[:].bitcast(F16)))
        m.dve_wait_given(dve)

    def stage_pe(self, pe, qd, p, k):
        m = self.misc
        m.pe_take(pe)
        pe.wait_ge(self.w_ready, 4 * qd + p + 1)
        w = (self.wa, self.wb)[k][:].rearrange("p t h v d -> p t (h v d)")
        out = m.bank[:].bitcast(F16)
        for t in range(8):
            last = self.nc.tensor.transpose(out[:, t * P:(t + 1) * P], w[:, t, :], self.r.ident16[:])
        m.pe_give(last)

    def switch_dve(self, dve, qd):
        v = self.nc.vector
        if not isinstance(qd, int) or qd > 0:
            dve.wait_ge(self.sc_ready, qd * (QPAIRS * self.STEPS))
        v.tensor_copy(self.a[:], self.a_next[:]).then_inc(self.a_switched, 1)
        dve.wait_ge(self.pv_done, qd * (UNITS * self.UNIT) + self.PV_START)
        v.tensor_copy(self.v[:], self.v_next[:]).then_inc(self.v_switched, 1)

    def unit_dve(self, s, u):
        v = self.nc.vector
        col = ((u // UNITS) % 2) * TOK + (u % UNITS) * CHUNK
        for h in range(4):
            rows = slice(32 * h, 32 * h + 32)
            last = v.tensor_copy(self.bst[s][rows, h, :], self.b[rows, bass.ds(col, CHUNK)])
        last.then_inc(self.units_ready, 1)

    def finish_dve(self, dve, u, n, s, next_unit=None):
        v, m = self.nc.vector, self.misc
        dve.wait_ge(self.pv_done, u * self.UNIT + self.PV_START)
        v.tensor_copy(self.acc_sb[:], self.acc[:]).then_inc(self.acc_read, 1)
        if next_unit is not None:
            self.unit_dve(s, next_unit)
        m.dve_take(dve)
        o = m.bank[:].rearrange("p (a e) -> p a e", e=32)
        Steps(dve, self.dv_finish, u).link(v.reciprocal(self.rs[:].rearrange("p (a o) -> p a o", o=1), o[:, :, HD:HD + 1]))
        dve.wait_ge(self.ctx_stored[s], n * 16)
        ctx = self.ctx_t[s][:].rearrange("p t (h d) -> p (t h) d", d=HD)
        m.dve_give(v.tensor_tensor(ctx, o[:, :, 0:HD], bcast(self.rs[:], HD), ALU.mult))
        m.dve_wait_given(dve)
        dve.sem_inc(self.ctx_ready, 1)

    def finish_pe(self, pe, u):
        m = self.misc
        m.pe_take(pe)
        pe.wait_ge(self.acc_read, u + 1)
        for t in range(4):
            last = self.nc.tensor.transpose(m.bank[:, t * P:(t + 1) * P], self.acc_sb[:, t * P:(t + 1) * P], self.r.ident[:])
        m.pe_give(last)

    def store_ctx(self, sp, u, s):
        sp.wait_ge(self.ctx_ready, u + 2)
        qd, c = u // UNITS, u % UNITS
        dst = self.d.ctx[bass.ds((qd // QUADS) * TOK + c * CHUNK, CHUNK), bass.ds((qd % QUADS) * 32, 32)]
        sp.dma_start(dst.rearrange("(t p) c -> p t c", p=P), self.ctx_t[s][:]).then_inc(self.ctx_stored[s], 16)

    def scores(self, pe, k, s):
        t, hp = divmod(k % (self.STEPS // 2), 2)
        for i in range(2):
            last = self.nc.tensor.matmul(self.sc[k % self.SC][:, i, :], self.a[:, t * P:(t + 1) * P],
                                         self.bst[s][:, 2 * hp + i, :], start=True, stop=True)
        last.then_inc(self.sc_ready, 1)

    def values(self, pe, g, n):
        s, t = divmod(g, self.UNIT)
        if t == 0:
            pe.wait_ge(self.acc_read, 2 * n + s + 1)
            if s == 0:
                pe.wait_ge(self.v_switched, n // QPAIRS + 1)
        for h in range(4):
            e = self.e[(2 * g + h // 2) % self.NE]
            last = self.nc.tensor.matmul(self.acc[32 * h:32 * h + HD + 1, :], self.v[:, t, h, :], e[:, h % 2, :],
                                         start=(t == 0), stop=(t == self.UNIT - 1))
        last.then_inc(self.pv_done, 1)

    def first_scores(self, pe, n, a_need):
        pe.wait_ge(self.units_ready, 2 * n + 1)
        pe.wait_ge(self.a_switched, a_need)
        pe.wait_ge(self.exp_done, n * self.STEPS + 2)
        self.scores(pe, 0, 0)
        pe.wait_ge(self.exp_done, n * self.STEPS + 3)
        self.scores(pe, 1, 0)
        self.scores(pe, 2, 0)

    def pair_pe(self, pe, n, background, a_next_need):
        for k in range(3, self.STEPS):
            if k == self.STEPS // 2:
                pe.wait_ge(self.units_ready, 2 * n + 2)
            pe.wait_ge(self.exp_done, n * self.STEPS + (k + 1))
            self.scores(pe, k, k // (self.STEPS // 2))
            if k % 2 and k >= 5:
                self.values(pe, (k - 5) // 2, n)
            if k in background:
                background[k]()
        pe.wait_ge(self.exp_done, n * self.STEPS + (self.STEPS - 2 + self.SC))
        self.values(pe, 2 * self.UNIT - 2, n)
        self.first_scores(pe, n + 1, a_next_need)
        self.values(pe, 2 * self.UNIT - 1, n)

    def pair_act(self, act, n):
        base = n * self.STEPS
        for k in range(self.STEPS):
            act.wait_ge(self.sc_ready, base + (k + 1))
            if k % 2 == 0:
                act.wait_ge(self.pv_done, n * (2 * self.UNIT) + (k // 2 + 1))
            self.nc.scalar.activation(self.e[k % self.NE][:], self.sc[k % self.SC][:], ACT.Exp,
                                      scale=1.0 / HD ** 0.5).then_inc(self.exp_done, 1)



class FfnStep:

    ITEMS = 6
    DVE_STEPS = 77

    def __init__(self, nc, d, r, stack, misc):
        sb = lambda n, s, t=F32: stack.enter_context(nc.sbuf_tensor(n, s, t))
        sem = lambda n: stack.enter_context(nc.semaphore(n))
        self.nc, self.d, self.r, self.misc = nc, d, r, misc
        self.t1, self.ctx, self.xn, self.x1, self.y, self.tmp, self.t2 = (
            sb("f_" + n, [P, 2, P]) for n in ("t1", "ctx", "xn", "x1", "y", "tmp", "t2"))
        self.stat, self.ctx_t, self.zf = sb("f_stat", [P, 4, 2]), sb("f_ctx_t", [P, 2 * P]), sb("f_zf", [P, 2, HD + 1])
        self.z = [sb(f"f_z{i}", [P, 2, HD]) for i in range(4)]
        self.zf_t, self.h_t = sb("f_zf_t", [HD + 1, 2 * P]), sb("f_h_t", [P, 4, 2 * P])
        self.dv, self.loaded, self.t2_ready, self.stored, self.init = (
            sem(n) for n in ("ffn_dve", "ffn_loaded", "t2_ready", "t2_stored", "ffn_init"))

    def init_dve(self, dve):
        self.nc.vector.memset(self.zf[:], 1.0).then_inc(self.init, 1)
        dve.wait_ge(self.init, 1)

    def load_sp(self, sp, m):
        sp.wait_ge(self.t2_ready, m)
        sp.dma_start(self.t1[:], token_pair(self.d.t1, m)).then_inc(self.loaded, 16)
        sp.dma_start(self.ctx[:], token_pair(self.d.ctx, m)).then_inc(self.loaded, 16)

    def store_sp(self, sp, m):
        sp.wait_ge(self.t2_ready, m + 1)
        sp.dma_start(token_pair(self.d.t2, m), self.t2[:]).then_inc(self.stored, 16)

    def vec(self, i):
        return self.r.vecs[:, i:i + 1, :].to_broadcast([P, 2, P])

    def first_dve(self, dve, n):
        nc, m, r = self.nc, self.misc, self.r
        v = nc.vector
        st = self.st = Steps(dve, self.dv, n * self.DVE_STEPS)
        flat = lambda x: x[:].rearrange("p t c -> p (t c)")
        pair = m.bank[:, 0:2 * P].rearrange("p (t c) -> p t c", t=2)
        m.dve_take(dve)
        m.dve_give(v.tensor_copy(self.ctx_t[:], m.bank[:, 0:2 * P]))
        dve.wait_ge(self.loaded, (n + 1) * 32)
        layer_norm(nc, st, self.xn[:], self.t1[:], self.tmp[:], self.stat, 2, P, 1e-5)
        m.dve_take(dve)
        st.link(v.tensor_tensor(self.y[:], pair, self.vec(0), ALU.add))
        st.link(v.tensor_tensor(self.y[:], self.y[:], self.xn[:], ALU.add))
        layer_norm(nc, st, self.x1[:], self.y[:], self.tmp[:], self.stat, 2, P, 1e-5, r.vecs[:, 2, :], r.vecs[:, 3, :])
        z = [q[:] for q in self.z]
        st.link(v.tensor_copy(z[0], self.x1[:, :, 0:HD]))
        cosine(nc, st, *z)
        ry = r.cos_ry[:].rearrange("p (o w) -> p o w", o=1).to_broadcast([P, 2, HD])
        m.dve_give(v.tensor_tensor(self.zf[:, :, 0:HD], z[0], ry, ALU.mult))

    def second_dve(self, dve, n):
        nc, m, r, st = self.nc, self.misc, self.r, self.st
        v = nc.vector
        pair = m.bank[:, 0:2 * P].rearrange("p (t c) -> p t c", t=2)
        m.dve_take(dve)
        m.dve_give(v.tensor_copy(self.zf_t[:], m.bank[0:HD + 1, 0:2 * P]))
        for c in range(2):
            m.dve_take(dve)
            m.dve_give(v.tensor_scalar(self.h_t[:, 2 * c:2 * c + 2, :].rearrange("p c t -> p (c t)"), m.bank[:], 0.0, None, ALU.max))
        m.dve_take(dve)
        m.dve_give(v.tensor_tensor(self.y[:], pair, self.vec(1), ALU.add))
        m.dve_wait_given(dve)
        st.link(v.tensor_tensor(self.y[:], self.y[:], self.x1[:], ALU.add))
        layer_norm(nc, st, self.xn[:], self.y[:], self.tmp[:], self.stat, 2, P, 1e-5, r.vecs[:, 4, :], r.vecs[:, 5, :])
        dve.wait_ge(self.stored, n * 16)
        v.tensor_tensor(self.t2[:], self.xn[:], self.t1[:], ALU.add).then_inc(self.t2_ready, 1)
        assert st.n == self.DVE_STEPS, st.n

    def item_pe(self, pe, n, i):
        nc, m, r = self.nc, self.misc, self.r
        T = nc.tensor
        m.pe_take(pe)
        if i == 0:
            pe.wait_ge(self.loaded, (n + 1) * 32)
            for t in range(2):
                last = T.transpose(m.bank[:, t * P:(t + 1) * P], self.ctx[:, t, :], r.ident[:])
        elif i == 1:
            for t in range(2):
                last = T.matmul(m.bank[:, t * P:(t + 1) * P], self.ctx_t[:, t * P:(t + 1) * P], r.combw[:], start=True, stop=True)
        elif i == 2:
            for t in range(2):
                last = T.transpose(m.bank[0:HD + 1, t * P:(t + 1) * P], self.zf[:, t, :], r.ident[:])
        elif i in (3, 4):
            for c in range(2):
                ffn = (2 * (i - 3) + c) * P
                last = T.matmul(m.bank[:, c * 2 * P:(c + 1) * 2 * P], r.w1[:, ffn:ffn + P], self.zf_t[:], start=True, stop=True)
        else:
            for t in range(2):
                for c in range(4):
                    last = T.matmul(m.bank[:, t * P:(t + 1) * P], self.h_t[:, c, t * P:(t + 1) * P], r.w2[:, c, :],
                                    start=(c == 0), stop=(c == 3))
        m.pe_give(last)


LEAD, LAG = 20, 16


def stage_main(nc, d, r, stack):
    misc = Misc(stack.enter_context(nc.psum_tensor("misc", [P, 512], F32)),
                stack.enter_context(nc.semaphore("misc_full")), stack.enter_context(nc.semaphore("misc_free")))
    conv, at, ffn = ConvStep(nc, d, r, stack, misc), AttnStep(nc, d, r, stack, misc), FfnStep(nc, d, r, stack, misc)
    block = stack.enter_context(nc.Block())
    ctx_there = stack.enter_context(nc.semaphore("ctx_there"))
    QUADRUPLES = IMAGES * QUADS
    SEGMENTS, at_misc = [], LEAD * 8 + QPAIRS * 2
    for q0, q1 in ((0, 4), (4, 11), (11, 15), (15, 16)):
        has_conv, has_ffn, follows = q1 <= (PAIRS - LEAD) // QPAIRS, q0 >= LAG // QPAIRS, q1 < QUADRUPLES
        per = 2 + 8 * has_conv + FfnStep.ITEMS * has_ffn + 2 * follows
        SEGMENTS.append((q0, q1, has_conv, has_ffn, follows, at_misc - q0 * QPAIRS * per, per))
        at_misc += (q1 - q0) * QPAIRS * per

    @block.sync
    def _(sp):
        with sp.Fori(0, LEAD) as n:
            conv.load_sp(sp, n)
            conv.store_sp(sp, n)
        sp.wait_ge(conv.stored, LEAD * 48)
        at.load_q(sp, 0)
        sp.sem_inc(at.ctx_stored[1], 16)
        for q0, q1, has_conv, has_ffn, follows, _, _ in SEGMENTS:
            with sp.Fori(q0, q1) as qd:
                if follows:
                    if has_conv:
                        sp.wait_ge(conv.stored, (qd * QPAIRS + LEAD) * 48)
                    else:
                        sp.wait_ge(conv.stored, PAIRS * 48)
                    at.load_q(sp, qd + 1)
                with sp.Fori(0, QPAIRS) as p:
                    n = qd * QPAIRS + p
                    if has_conv:
                        conv.load_sp(sp, n + LEAD)
                    if has_ffn:
                        for s in range(2):
                            sp.wait_ge(at.ctx_stored[s], n * 16 - 32 + 16 * s)
                            sp.sem_inc(ctx_there, 1)
                        ffn.load_sp(sp, n - LAG)
                    at.store_ctx(sp, 2 * n, 0)
                    if has_ffn:
                        ffn.store_sp(sp, n - LAG)
                    if has_conv:
                        conv.store_sp(sp, n + LEAD)
                    at.store_ctx(sp, 2 * n + 1, 1)
        for s in range(2):
            sp.wait_ge(at.ctx_stored[s], (PAIRS + s) * 16)
        with sp.Fori(PAIRS - LAG, PAIRS) as m:
            ffn.load_sp(sp, m)
            ffn.store_sp(sp, m)
        sp.wait_ge(ffn.stored, PAIRS * 16)

    @block.gpsimd
    def _(pool):
        with pool.Fori(0, PAIRS) as n:
            conv.pool(pool, n)

    @block.scalar
    def _(act):
        act.sem_inc(at.exp_done, at.SC)
        with act.Fori(0, PAIRS) as n:
            at.pair_act(act, n)

    @block.vector
    def _(dve):
        dve.sem_inc(misc.free, 1)
        dve.sem_inc(conv.val_ready, 2)
        for s in range(2):
            conv.stage_dve(dve, 0, s)
        at.init_dve(dve)
        ffn.init_dve(dve)
        with dve.Fori(0, LEAD) as n:
            misc.start(n * 8)
            st = Steps(dve, conv.dv, n * conv.STEPS)
            for s in range(2):
                conv.sample_dve(dve, n, s, st)
            for s in range(2):
                conv.product_dve(dve, n, s)
            conv.ring_dve(dve, n, st)
            assert st.n == conv.STEPS, st.n
        with dve.Fori(0, QPAIRS) as p:
            misc.start(LEAD * 8 + p * 2)
            at.stage_dve(dve, 0, p)
        at.unit_dve(0, 0)
        for q0, q1, has_conv, has_ffn, follows, misc0, per in SEGMENTS:
            with dve.Fori(q0, q1) as qd:
                at.switch_dve(dve, qd)
                with dve.Fori(0, QPAIRS) as p:
                    n = qd * QPAIRS + p
                    misc.start(n * per + misc0)
                    at.finish_dve(dve, 2 * n, n, 1, 2 * n + 1)
                    if has_ffn:
                        ffn.first_dve(dve, n - LAG)
                    if follows:
                        at.stage_dve(dve, qd + 1, p)
                    if has_conv:
                        st = Steps(dve, conv.dv, (n + LEAD) * conv.STEPS)
                        for s in range(2):
                            conv.sample_dve(dve, n + LEAD, s, st)
                        for s in range(2):
                            conv.product_dve(dve, n + LEAD, s)
                    at.finish_dve(dve, 2 * n + 1, n, 0, 2 * n + 2)
                    if has_ffn:
                        ffn.second_dve(dve, n - LAG)
                    if has_conv:
                        conv.ring_dve(dve, n + LEAD, st)
                    assert misc.d == per
        misc.start(at_misc)
        at.finish_dve(dve, 2 * PAIRS, PAIRS, 1)
        with dve.Fori(PAIRS - LAG, PAIRS) as m:
            misc.start((m - (PAIRS - LAG)) * FfnStep.ITEMS + at_misc + 1)
            ffn.first_dve(dve, m)
            ffn.second_dve(dve, m)

    @block.tensor
    def _(pe):
        with pe.Fori(0, LEAD) as n:
            misc.start(n * 8)
            for s in range(2):
                for item in conv.items_pe(pe, n, s):
                    item()
        with pe.Fori(0, QPAIRS) as p:
            misc.start(LEAD * 8 + p * 2)
            for k in range(2):
                at.stage_pe(pe, 0, p, k)
        pe.sem_inc(at.pv_done, at.PV_START)
        at.first_scores(pe, 0, 1)
        for q0, q1, has_conv, has_ffn, follows, misc0, per in SEGMENTS:
            with pe.Fori(q0, q1) as qd:
                with pe.Fori(0, QPAIRS) as p:
                    n = qd * QPAIRS + p
                    misc.start(n * per + misc0)
                    bg = {6: lambda: at.finish_pe(pe, 2 * n), 70: lambda: at.finish_pe(pe, 2 * n + 1)}
                    if has_ffn:
                        for i, k in enumerate((9, 12, 74, 77, 80, 83)):
                            bg[k] = lambda i=i: ffn.item_pe(pe, n - LAG, i)
                    if follows:
                        bg[26] = lambda: at.stage_pe(pe, qd + 1, p, 0)
                        bg[29] = lambda: at.stage_pe(pe, qd + 1, p, 1)
                    if has_conv:
                        for s, k0 in ((0, 43), (1, 51)):
                            for item, dk in zip(conv.items_pe(pe, n + LEAD, s), (0, 2, 4, 5, 6, 7)):
                                bg[k0 + dk] = item
                    at.pair_pe(pe, n, bg, (n + 1) // QPAIRS + 1 if follows else QUADRUPLES)
                    assert misc.p == per
        misc.start(at_misc)
        at.finish_pe(pe, 2 * PAIRS)
        with pe.Fori(PAIRS - LAG, PAIRS) as m:
            misc.start((m - (PAIRS - LAG)) * FfnStep.ITEMS + at_misc + 1)
            for i in range(FfnStep.ITEMS):
                ffn.item_pe(pe, m, i)



EXPERTS_AT_ONCE = 4
SLOTS = 2


def stage_experts(nc, d, ident, stack):
    sb = lambda n, s, t=F32: stack.enter_context(nc.sbuf_tensor(n, s, t))
    ps = lambda n: stack.enter_context(nc.psum_tensor(n, [P, 512], F32))
    sem = lambda n: stack.enter_context(nc.semaphore(n))
    DUOS, CHUNKS = IMAGES // 2, TOK // 512
    xn = [sb(f"xn_tok{i}", [P, TILES, P]) for i in range(2)]
    big, xn_t, logits, s_t = sb("e_big", [P, TOK]), sb("xn_ch", [P, TOK]), sb("logits", [P, TOK]), sb("s_tok", [P, TILES, P])
    sel = [sb(f"selected{i}", [P, TOK]) for i in range(DUOS)]
    stat, top, nmax, total, share = sb("e_stat", [P, 4, TILES]), sb("top", [P, TOPK]), sb("nmax", [P, 1]), sb("total", [P, 1]), sb("share", [P, 1])
    gatew, gateb = sb("gatew", [P, NEXP]), sb("gateb", [P, 1])
    b1, b2, b1_t, b2_t = sb("b1", [NEXP, 512]), sb("b2", [NEXP, P]), sb("b1_t", [P, NEXP, 4]), sb("b2_t", [P, NEXP])
    w1 = [sb(f"ew1_{i}", [P, EXPERTS_AT_ONCE, 512]) for i in range(SLOTS)]
    w2 = [sb(f"ew2_{i}", [P, EXPERTS_AT_ONCE, 4, P]) for i in range(SLOTS)]
    pooled, pooled_g = sb("pooled", [P, NEXP, IMAGES]), [sb(f"pooled_g{i}", [P, EXPERTS_AT_ONCE, IMAGES]) for i in range(SLOTS)]
    hb = [sb(f"hb{i}", [P, EXPERTS_AT_ONCE, 4, IMAGES]) for i in range(SLOTS)]
    hg = [sb(f"hg{i}", [P, EXPERTS_AT_ONCE, 4, IMAGES]) for i in range(SLOTS)]
    out_t, out_e = sb("out_t", [P, IMAGES, NEXP]), [sb(f"out_e{i}", [P, P]) for i in range(DUOS)]
    y = [sb(f"y{i}", [P, 512]) for i in range(2)]
    ps_t, ps_l = [ps(f"eps_t{i}") for i in range(2)], [ps(f"eps_l{i}") for i in range(2)]
    ps_p, ps_h, ps_o, ps_b = ps("eps_p"), ps("eps_h"), ps("eps_o"), ps("eps_b")
    (consts, biases, tr_full, tr_free, lg_full, lg_free, xn_ready, ex_ready, s_ready, st_full, pool_full, pool_free, top_ready,
     dv, bias_full, bias_done, pg_ready, h_full, hb_ready, hg_ready, o_full, o_done, oe_full, oe_done, y_full, y_free) = (
        sem(n) for n in ("e_consts", "e_biases", "e_tr_full", "e_tr_free", "lg_full", "lg_free", "xn_ready", "ex_ready", "s_ready",
                         "st_full", "pool_full", "pool_free", "top_ready", "e_dve", "bias_full", "bias_done", "pg_ready", "h_full",
                         "hb_ready", "hg_ready", "o_full", "o_done", "oe_full", "oe_done", "y_full", "y_free"))
    x_in = [sem(f"e_x_in{i}") for i in range(2)]
    w_in = [sem(f"w_in{i}") for i in range(SLOTS)]
    y_out = [sem(f"y_out{i}") for i in range(2)]
    NG = NEXP // EXPERTS_AT_ONCE
    block = stack.enter_context(nc.Block())

    tokens = lambda b: d.t2[b * TOK:(b + 1) * TOK, :].rearrange("(t p) c -> p t c", p=P)

    def stores(sp, b):
        for c in range(CHUNKS):
            sp.wait_ge(y_free, b * CHUNKS + c + 1)
            sp.dma_start(d.out[b, :, c * 512:(c + 1) * 512], y[c % 2][:]).then_inc(y_out[c % 2], 16)

    @block.sync
    def _(sp):
        sp.dma_start(gatew[:], d.gatew).then_inc(consts, 16)
        sp.dma_start(gateb[:], d.gateb).then_inc(consts, 16)
        for b in range(2):
            sp.dma_start(xn[b][:], tokens(b)).then_inc(x_in[b], 16)
        sp.dma_start(b1[:], d.ew1[:, P:P + 1, :].rearrange("e o h -> (e o) h")).then_inc(biases, 16)
        sp.dma_start(b2[:], d.ew2[:, 512:513, :].rearrange("e o h -> (e o) h")).then_inc(biases, 16)

        def weights(g, s):
            e = bass.ds(g * EXPERTS_AT_ONCE, EXPERTS_AT_ONCE)
            sp.dma_start(w1[s][:], d.ew1[e, 0:P, :].rearrange("e p h -> p e h")).then_inc(w_in[s], 16)
            for x in range(EXPERTS_AT_ONCE):
                sp.dma_start(w2[s][:, x], d.ew2[bass.ds(g * EXPERTS_AT_ONCE + x, 1), 0:512, :].rearrange("o (c p) h -> p (o c) h", p=P)).then_inc(w_in[s], 16)

        for g in range(SLOTS):
            weights(g, g)
        for b in range(2, IMAGES):
            sp.wait_ge(pool_full, b - 1)
            sp.dma_start(xn[b % 2][:], tokens(b)).then_inc(x_in[b % 2], 16)
        with sp.Fori(1, NG // SLOTS) as i:
            for s in range(SLOTS):
                sp.wait_ge(o_full, (i - 1) * SLOTS + s + 1)
                weights(i * SLOTS + s, s)
        for b in range(IMAGES):
            sp.wait_ge(pool_full, IMAGES) if b < 2 else sp.wait_ge(y_full, (b - 1) * CHUNKS)
            sp.dma_start(xn[b % 2][:], tokens(b)).then_inc(x_in[b % 2], 16)
            if b:
                stores(sp, b - 1)
        stores(sp, IMAGES - 1)
        for i in range(2):
            sp.wait_ge(y_out[i], IMAGES * CHUNKS // 2 * 16)

    @block.vector
    def _(dve):
        v = nc.vector
        st = Steps(dve, dv)
        for duo in range(DUOS):
            for i in range(2):
                dve.wait_ge(x_in[i], (duo + 1) * 16)
                layer_norm(nc, st, xn[i][:], xn[i][:], big[:].rearrange("p (t c) -> p t c", c=P), stat, TILES, P, 1e-5)
                dve.sem_inc(xn_ready, 1)
            for k in range(2 * CHUNKS):
                half = slice(NEXP * (k // CHUNKS), NEXP * (k // CHUNKS) + NEXP)
                c = k % CHUNKS
                dve.wait_ge(lg_full, 2 * CHUNKS * duo + k + 1)
                if k == 0 and duo:
                    dve.wait_ge(ex_ready, duo)
                if k == 0:
                    dve.wait_ge(consts, 32)
                v.tensor_scalar(logits[half, c * 512:(c + 1) * 512], ps_l[k % 2][half, :], gateb[half, :], None, ALU.add).then_inc(lg_free, 1)
            dve.wait_ge(lg_free, 2 * CHUNKS * (duo + 1))
            st.link(v.max(top[:], logits[:]))
            v.tensor_scalar(nmax[:], top[:, 0:1], -1.0, None, ALU.mult).then_inc(top_ready, 1)
            st.link(v.match_replace(big[:], top[:], logits[:], -3.0e38))
            st.link(v.tensor_tensor(big[:], big[:], logits[:], ALU.not_equal))
            dve.wait_ge(ex_ready, duo + 1)
            st.link(v.reciprocal(share[:], total[:]))
            v.scalar_tensor_tensor(out=sel[duo][:], in0=xn_t[:], scalar=share[:], in1=big[:], op0=ALU.mult, op1=ALU.mult).then_inc(s_ready, 1)
            dve.wait_ge(s_ready, duo + 1)
            for i in range(2):
                b = 2 * duo + i
                dve.wait_ge(pool_full, b + 1)
                v.tensor_copy(pooled[:, :, b:b + 1], ps_p[:, 0:NEXP].rearrange("p (e o) -> p e o", o=1)).then_inc(pool_free, 1)
        dve.wait_ge(pool_free, IMAGES)
        dve.wait_ge(bias_full, 1)
        v.tensor_copy(b1_t[:], ps_b[:, 0:4 * NEXP].rearrange("p (c e) -> p e c", c=4)).then_inc(bias_done, 1)
        v.tensor_copy(b2_t[:], ps_b[:, 4 * NEXP:5 * NEXP]).then_inc(bias_done, 1)
        dve.wait_ge(bias_done, 2)
        with dve.Fori(0, NG // SLOTS) as i:
            for s in range(SLOTS):
                g = i * SLOTS + s
                es = bass.ds(g * EXPERTS_AT_ONCE, EXPERTS_AT_ONCE)
                v.tensor_copy(pooled_g[s][:], pooled[:, es, :]).then_inc(pg_ready, 1)
                dve.wait_ge(h_full, g + 1)
                v.tensor_tensor(hb[s][:].rearrange("p e c b -> p (e c) b"), ps_h[:, 0:16 * EXPERTS_AT_ONCE].rearrange("p (a b) -> p a b", b=IMAGES),
                                bcast(b1_t[:, es, :].rearrange("p e c -> p (e c)"), IMAGES), ALU.add).then_inc(hb_ready, 1)
                dve.wait_ge(o_full, g + 1)
                v.tensor_tensor(out_t[:, :, es], ps_o[:, 0:4 * EXPERTS_AT_ONCE].rearrange("p (e b) -> p b e", b=IMAGES),
                                b2_t[:, es].rearrange("p (o e) -> p o e", o=1).to_broadcast([P, IMAGES, EXPERTS_AT_ONCE]), ALU.add).then_inc(o_done, 1)
        for duo in range(DUOS):
            dve.wait_ge(oe_full, duo + 1)
            v.tensor_copy(out_e[duo][:], ps_t[duo][:, 0:P]).then_inc(oe_done, 1)
        for n in range(IMAGES * CHUNKS):
            dve.wait_ge(y_full, n + 1)
            if n >= 2:
                dve.wait_ge(y_out[n % 2], n // 2 * 16)
            v.tensor_copy(y[n % 2][:], ps_l[n % 2][:]).then_inc(y_free, 1)

    @block.scalar
    def _(act):
        n = 0
        for duo in range(DUOS):
            for i in range(2):
                for g in range(CHUNKS):
                    act.wait_ge(tr_full, n + 1)
                    if g == 0 and i == 0 and duo:
                        act.wait_ge(s_ready, duo)
                    if g == 0 and i == 1:
                        act.wait_ge(lg_full, 2 * CHUNKS * duo + CHUNKS)
                    nc.scalar.copy(xn_t[:, g * 512:(g + 1) * 512], ps_t[n % 2][:]).then_inc(tr_free, 1)
                    n += 1
            act.wait_ge(top_ready, duo + 1)
            act.wait_ge(lg_full, 2 * CHUNKS * (duo + 1))
            nc.scalar.activation(xn_t[:], logits[:], ACT.Exp, bias=nmax[:], accum_out=total[:]).then_inc(ex_ready, 1)
            for g in range(CHUNKS):
                act.wait_ge(tr_full, n + 1)
                nc.scalar.copy(s_t[:, 4 * g:4 * g + 4, :].rearrange("p t c -> p (t c)"), ps_t[n % 2][:]).then_inc(tr_free, 1)
                n += 1
        with act.Fori(0, NG // SLOTS) as i:
            for s in range(SLOTS):
                act.wait_ge(hb_ready, i * SLOTS + s + 1)
                nc.scalar.activation(hg[s][:], hb[s][:], ACT.Gelu).then_inc(hg_ready, 1)

    @block.tensor
    def _(pe):
        T = nc.tensor
        n = 0
        for duo in range(DUOS):
            for i in range(2):
                pe.wait_ge(xn_ready, 2 * duo + i + 1)
                for g in range(CHUNKS):
                    if n >= 2:
                        pe.wait_ge(tr_free, n - 1)
                    for j in range(4):
                        last = T.transpose(ps_t[n % 2][:, j * P:(j + 1) * P], xn[i][:, 4 * g + j, :], ident[:])
                    last.then_inc(tr_full, 1)
                    n += 1
                for c in range(CHUNKS):
                    k = 2 * CHUNKS * duo + CHUNKS * i + c
                    pe.wait_ge(tr_free, n - CHUNKS + c + 1)
                    if k == 0:
                        pe.wait_ge(consts, 32)
                    if k >= 2:
                        pe.wait_ge(lg_free, k - 1)
                    T.matmul(ps_l[c % 2][NEXP * i:NEXP * (i + 1), :], gatew[:], xn_t[:, c * 512:(c + 1) * 512], start=True, stop=True).then_inc(lg_full, 1)
            pe.wait_ge(s_ready, duo + 1)
            for g in range(CHUNKS):
                pe.wait_ge(tr_free, n - 1)
                for j in range(4):
                    t = 4 * g + j
                    last = T.transpose(ps_t[n % 2][:, j * P:(j + 1) * P], sel[duo][:, t * P:(t + 1) * P], ident[:])
                last.then_inc(tr_full, 1)
                n += 1
            pe.wait_ge(tr_free, n)
            for i in range(2):
                b = 2 * duo + i
                if b:
                    pe.wait_ge(pool_free, b)
                for t in range(TILES):
                    last = T.matmul(ps_p[:, 0:NEXP], xn[i][:, t, :], s_t[:, t, NEXP * i:NEXP * (i + 1)], start=(t == 0), stop=(t == TILES - 1))
                last.then_inc(pool_full, 1)
        pe.wait_ge(biases, 32)
        for c in range(4):
            T.transpose(ps_b[:, c * NEXP:(c + 1) * NEXP], b1[:, c * P:(c + 1) * P], ident[0:NEXP, 0:NEXP])
        T.transpose(ps_b[:, 4 * NEXP:5 * NEXP], b2[:], ident[0:NEXP, 0:NEXP]).then_inc(bias_full, 1)
        with pe.Fori(0, NG // SLOTS) as i:
            for s in range(SLOTS):
                g = i * SLOTS + s
                pe.wait_ge(w_in[s], (i + 1) * 16 * (1 + EXPERTS_AT_ONCE))
                pe.wait_ge(pg_ready, g + 1)
                pe.wait_ge(hb_ready, g)
                for e in range(EXPERTS_AT_ONCE):
                    for c in range(4):
                        at = (4 * e + c) * IMAGES
                        last = T.matmul(ps_h[:, at:at + IMAGES], w1[s][:, e, c * P:(c + 1) * P], pooled_g[s][:, e, :], start=True, stop=True)
                last.then_inc(h_full, 1)
                pe.wait_ge(hg_ready, g + 1)
                pe.wait_ge(o_done, g)
                for e in range(EXPERTS_AT_ONCE):
                    for c in range(4):
                        last = T.matmul(ps_o[:, e * IMAGES:(e + 1) * IMAGES], w2[s][:, e, c, :], hg[s][:, e, c, :], start=(c == 0), stop=(c == 3))
                last.then_inc(o_full, 1)
        pe.wait_ge(o_done, NG)
        for duo in range(DUOS):
            T.transpose(ps_t[duo][:, 0:P], out_t[:, 2 * duo:2 * duo + 2, :].rearrange("p b e -> p (b e)"), ident[:]).then_inc(oe_full, 1)
        pe.wait_ge(oe_done, DUOS)
        for b in range(IMAGES):
            pe.wait_ge(x_in[b % 2], (DUOS + b // 2 + 1) * 16)
            half = slice(NEXP * (b % 2), NEXP * (b % 2 + 1))
            for c in range(CHUNKS):
                n = b * CHUNKS + c
                if n >= 2:
                    pe.wait_ge(y_free, n - 1)
                T.matmul(ps_l[c % 2][:], out_e[b // 2][half, :], sel[b // 2][half, c * 512:(c + 1) * 512], start=True, stop=False)
                for j in range(4):
                    last = T.matmul(ps_l[c % 2][:, j * P:(j + 1) * P], xn[b % 2][:, 4 * c + j, :], ident[:], start=False, stop=(j == 3))
                last.then_inc(y_full, 1)


class Views:

    def __init__(self, nc, arrays, kinds):
        view = {k: nc.dram_tensor("in_" + k, v.shape, mybir.dt.from_np(v.dtype), kind="ExternalInput").ap()
                for k, v in arrays.items()}
        self.x, self.x_tok, self.offw, self.offb, self.dcnw = (view[k] for k in ("x", "x_tok", "offw", "offb", "dcnw"))
        self.base, self.gmat, self.gatew, self.gateb = (view[k] for k in ("base", "gmat", "gatew", "gateb"))
        self.ew1, self.ew2 = view["ew1"], view["ew2"]
        self.shared = {k: view[k] for k in SHARED}
        inner = lambda name, shape: nc.dram_tensor(name, shape, F32, kind=kinds.get(name, "Internal")).ap()
        self.table = inner("table", (IMAGES * TROWS, 4 * P))
        self.t1 = inner("t1", (IMAGES * TOK, CH))
        self.q = inner("q", (QUADS, IMAGES * TOK, 4 * HD))
        self.ctx = inner("ctx", (IMAGES * TOK, CH))
        self.t2 = inner("t2", (IMAGES * TOK, CH))
        self.out = nc.dram_tensor("out", (IMAGES, CH, TOK), F32, kind="ExternalOutput").ap()


class Shared:

    def __init__(self, nc, stack, ident):
        sb = lambda n, s, t=F32: stack.enter_context(nc.sbuf_tensor(n, s, t))
        self.ident = ident
        self.idx = sb("idx", [P, IMAGES * TILES * TAPS], I32)
        self.wts = sb("wts", [P, IMAGES * TILES, TAPS, 4])
        self.ident16 = sb("ident16", [P, P], F16)
        self.image_row, self.theta, self.dcnw = sb("image_row", [P, IMAGES]), sb("theta", [P, P]), sb("dcnw", [P, TAPS, P])
        self.combw, self.vecs, self.w1 = sb("combw", [P, P]), sb("vecs", [P, 6, P]), sb("w1", [HD + 1, FFN])
        self.w2, self.cos_ry = sb("w2", [P, 4, P]), sb("cos_ry", [P, HD])


def host_layout(inputs):
    a = {k: np.asarray(v) for k, v in inputs.items()}
    rep = lambda v: np.tile(v.reshape(1, -1), (P, 1))
    x = a["x"].reshape(IMAGES, CH, TOK)
    p = np.arange(P)
    tile_y = 2 * np.arange(TILES)[None, :, None] + (p // SIDE)[:, None, None] + (np.arange(TAPS) // 3)[None, None, :]
    tile_x = (p % SIDE)[:, None, None] + 0 * np.arange(TILES)[None, :, None] + (np.arange(TAPS) % 3)[None, None, :]
    out = {
        "x": x,
        "x_tok": x.transpose(0, 2, 1).reshape(IMAGES * TOK, CH),
        "offw": a["L0_conv_offset_w"].reshape(27, CH, TAPS).transpose(1, 2, 0),
        "offb": rep(a["L0_conv_offset_b"]),
        "dcnw": a["L0_conv_dcn_w"].reshape(CH, CH, TAPS).transpose(1, 2, 0),
        "base": np.stack([tile_y, tile_x], 1).astype(np.float32),
        "gmat": np.kron(np.eye(32), np.full((4, 4), 0.25)).astype(np.float32),
        "ident": np.eye(P, dtype=np.float32),
        "image_row": rep(np.arange(IMAGES) * TROWS + MARGIN).astype(np.float32),
        "theta": rep(np.tile(a["L1_attn_rx_theta"], HEADS)),
        "ry": rep(a["L1_attn_ry_theta"]),
        "combw": a["L1_attn_w_comb"].T,
        "vecs": np.stack([rep(a["L1_attn_" + n]) for n in ("b_comb", "b2", "g1", "beta1", "g2", "beta2")], 1),
        "w1": np.concatenate([a["L1_attn_w1"].T, a["L1_attn_b1"][None]], 0),
        "w2": a["L1_attn_w2"].T.reshape(4, P, CH).transpose(1, 0, 2),
        "gatew": a["L1_ffn_gate_w"].T,
        "gateb": np.tile(a["L1_ffn_gate_b"], 2)[:, None],
        "ew1": a["L1_ffn_weight1"],
        "ew2": a["L1_ffn_weight2"],
    }
    return {k: np.ascontiguousarray(v) for k, v in out.items()}


SHARED = ("ident", "image_row", "theta", "dcnw", "combw", "vecs", "w1", "w2", "ry")


def build(nc, arrays, stages=("offsets", "main", "experts"), kinds={}):
    d = Views(nc, arrays, kinds)
    with ExitStack() as whole:
        ident = whole.enter_context(nc.sbuf_tensor("ident", [P, P], F32))
        with ExitStack() as body:
            r = Shared(nc, body, ident)
            stage_constants(nc, d, r, body)
            if "offsets" in stages:
                with ExitStack() as st:
                    stage_offsets(nc, d, r, st)
            if "main" in stages:
                with ExitStack() as st:
                    stage_main(nc, d, r, st)
        if "experts" in stages:
            with ExitStack() as st:
                stage_experts(nc, d, ident, st)


def stage_constants(nc, d, r, stack):
    places = (r.ident, r.image_row, r.theta, r.dcnw, r.combw, r.vecs, r.w1, r.w2, r.cos_ry)
    scratch = [stack.enter_context(nc.sbuf_tensor(f"ry{i}", [P, HD], F32)) for i in range(3)]
    with ExitStack() as s:
        loaded, dv = (s.enter_context(nc.semaphore(n)) for n in ("shared_loaded", "shared_dve"))
        block = s.enter_context(nc.Block())

        @block.sync
        def _(sp):
            for place, name in zip(places, SHARED):
                sp.dma_start(place[:], d.shared[name]).then_inc(loaded, 16)
            sp.wait_ge(loaded, 16 * len(places))

        @block.vector
        def _(dve):
            dve.wait_ge(loaded, 16 * len(places))
            st = Steps(dve, dv)
            st.link(nc.vector.tensor_copy(r.ident16[:], r.ident[:]))
            cosine(nc, st, r.cos_ry[:], *(q[:] for q in scratch))


def kernel(**inputs):
    from concourse import bacc
    from concourse.bass_utils import run_bass_kernel_spmd

    arrays = host_layout(inputs)
    nc = bacc.Bacc("TRN2", target_bir_lowering=False, num_devices=1)
    build(nc, arrays)
    result = run_bass_kernel_spmd(nc, [{"in_" + k: v for k, v in arrays.items()}], core_ids=[0])
    return result.results[0]["out"].reshape(IMAGES, CH, SIDE, SIDE)
```

```python
from contextlib import ExitStack

import numpy as np
import concourse.bass as bass
from concourse import mybir

F32 = mybir.dt.float32
F16 = mybir.dt.float16
BF16 = mybir.dt.bfloat16
I32 = mybir.dt.int32
ALU = mybir.AluOpType
ACT = mybir.ActivationFunctionType
AX = mybir.AxisListType.X

P = 128
IMAGES, CH, SIDE = 4, 128, 64
TOK = SIDE * SIDE
TILES = TOK // P
TAPS = 9
PADW = SIDE + 3
NPAD = 36
PADPIX = NPAD * P
MARGIN = 128
TROWS = MARGIN + PADPIX
CORNERS = (0, 1, PADW, PADW + 1)
HEADS, HD = 16, 8
QUADS = HEADS // 4
CHUNK = 512
UNITS = TOK // CHUNK
FFN = 512
NEXP, TOPK = 64, 8
PAIRS = IMAGES * TILES // 2
QPAIRS = UNITS // 2
MAGIC = 12582912.0
TWO_PI_HI, TWO_PI_LO = 6.28125, 0.0019353071795864769
RSQRT_SEED = 1597463007.0
SIN_HALF = [(-1) ** k / (2.0 ** (2 * k + 1)) / float(np.prod(np.arange(1, 2 * k + 2, dtype=np.float64))) for k in range(8)]


class Steps:

    def __init__(self, eng, sem, base=0):
        self.eng, self.sem, self.base, self.n = eng, sem, base, 0

    def inc(self, ins):
        self.n += 1
        return ins.then_inc(self.sem, 1)

    def wait(self, eng=None, back=0):
        (eng or self.eng).wait_ge(self.sem, self.base + (self.n - back))

    def link(self, ins):
        self.inc(ins)
        self.wait()


def bcast(ap2, n):
    return ap2.rearrange("p (a o) -> p a o", o=1).to_broadcast([ap2.shape[0], ap2.shape[1], n])


def layer_norm(nc, st, out, x, tmp, stat, n, w, eps, gain=None, shift=None):
    v = nc.vector
    s, m, y, b = stat[:, 0, 0:n], stat[:, 1, 0:n], stat[:, 2, 0:n], stat[:, 3, 0:n]
    st.link(v.tensor_reduce(s, x, AX, ALU.add))
    st.link(v.tensor_scalar(m, s, 1.0 / w, None, ALU.mult))
    st.link(v.tensor_tensor(out, x, bcast(m, w), ALU.subtract))
    st.link(v.tensor_tensor(tmp, out, out, ALU.mult))
    st.link(v.tensor_reduce(s, tmp, AX, ALU.add))
    st.link(v.tensor_scalar(s, s, 1.0 / w, eps, ALU.mult, ALU.add))
    rsqrt(nc, st, y, s, m, b)
    st.link(v.tensor_tensor(out, out, bcast(y, w), ALU.mult))
    if gain is not None:
        p = x.shape[0]
        g = gain.rearrange("p (o w) -> p o w", o=1).to_broadcast([p, n, w])
        h = shift.rearrange("p (o w) -> p o w", o=1).to_broadcast([p, n, w])
        st.link(v.tensor_tensor(out, out, g, ALU.mult))
        st.link(v.tensor_tensor(out, out, h, ALU.add))


def rsqrt(nc, st, y, x, a, b):
    v = nc.vector
    st.link(v.tensor_scalar(a.bitcast(I32), x.bitcast(I32), 1, None, ALU.logical_shift_right))
    st.link(v.tensor_scalar(y.bitcast(I32), a.bitcast(I32), -1.0, RSQRT_SEED, ALU.mult, ALU.add))
    for _ in range(3):
        st.link(v.scalar_tensor_tensor(out=a, in0=y, scalar=-0.5, in1=y, op0=ALU.mult, op1=ALU.mult))
        st.link(v.tensor_tensor(b, a, x, ALU.mult))
        st.link(v.scalar_tensor_tensor(out=y, in0=b, scalar=1.5, in1=y, op0=ALU.add, op1=ALU.mult))


def cosine(nc, st, x, k, z, p):
    v = nc.vector
    st.link(v.tensor_scalar(k, x, 1.0 / (2 * np.pi), MAGIC, ALU.mult, ALU.add))
    st.link(v.tensor_scalar(k, k, MAGIC, None, ALU.subtract))
    st.link(v.scalar_tensor_tensor(out=x, in0=k, scalar=-TWO_PI_HI, in1=x, op0=ALU.mult, op1=ALU.add))
    st.link(v.scalar_tensor_tensor(out=x, in0=k, scalar=-TWO_PI_LO, in1=x, op0=ALU.mult, op1=ALU.add))
    st.link(v.tensor_tensor(z, x, x, ALU.mult))
    st.link(v.tensor_scalar(p, z, SIN_HALF[-1], SIN_HALF[-2], ALU.mult, ALU.add))
    st.link(v.tensor_tensor(p, p, z, ALU.mult))
    for c in SIN_HALF[-3:0:-1]:
        st.link(v.scalar_tensor_tensor(out=p, in0=p, scalar=c, in1=z, op0=ALU.add, op1=ALU.mult))
    st.link(v.scalar_tensor_tensor(out=p, in0=p, scalar=SIN_HALF[0], in1=x, op0=ALU.add, op1=ALU.mult))
    st.link(v.scalar_tensor_tensor(out=z, in0=p, scalar=-2.0, in1=p, op0=ALU.mult, op1=ALU.mult))
    st.link(v.tensor_scalar(x, z, 1.0, None, ALU.add))


def stage_offsets(nc, d, r, stack):
    sb = lambda n, s, t=F32: stack.enter_context(nc.sbuf_tensor(n, s, t))
    sem = lambda n: stack.enter_context(nc.semaphore(n))
    SLOTS = 2
    GROUPS, OUTS = NPAD // 4, 3 * TAPS
    BANDS = SIDE // 8
    x_ch = [sb(f"x_ch{s}", [P, TOK]) for s in range(SLOTS)]
    pix = [sb(f"pix{s}", [P, NPAD, P]) for s in range(SLOTS)]
    xpad = sb("xpad", [P, PADPIX])
    zero = sb("zero", [P, 4 * P])
    om_ch = [sb(f"om_ch{h}", [P, 512]) for h in range(2)]
    om = sb("om", [P, TILES, OUTS])
    pos = [sb(f"pos{i}", [P, TILES, TAPS]) for i in range(6)]
    offw, offb, base, gmat = sb("offw", [P, TAPS, OUTS]), sb("offb", [P, 1]), sb("base", [P, 2, TILES, TAPS]), sb("gmat", [P, P])
    bn, agg, gs = sb("bn", [P, 8, 6]), sb("agg", [P, 2]), sb("gs", [P, 8])
    ps_conv = [stack.enter_context(nc.psum_tensor(f"ps_conv{h}", [P, 512], F32)) for h in range(2)]
    ps_om = stack.enter_context(nc.psum_tensor("ps_om", [P, 2, 512], F32))
    ps_t = stack.enter_context(nc.psum_tensor("ps_t", [P, 2, 512], F32))
    ps_g = stack.enter_context(nc.psum_tensor("ps_g", [P, 512], F32))
    consts, x_read, edges = sem("c1_consts"), sem("x_read"), sem("edges")
    x_loaded = [sem(f"x_loaded{s}") for s in range(SLOTS)]
    tables = [sem(f"tables{s}") for s in range(SLOTS)]
    dv, stat_ready, group_ready, padded, init = sem("c1_dve"), sem("stat_ready"), sem("group_ready"), sem("padded"), sem("c1_init")
    conv_full, conv_read, om_full, om_read, tr_full, tr_free = (
        sem(n) for n in ("conv_full", "conv_read", "om_full", "om_read", "tr_full", "tr_free"))
    sig, summed = sem("sig"), sem("summed")
    interior = xpad[:, 0:PADW * (SIDE + 2)].rearrange("p (y x) -> p y x", x=PADW)
    DVE_STEPS = 36

    block = stack.enter_context(nc.Block())

    @block.sync
    def _(sp):
        for b in range(SLOTS):
            sp.dma_start(x_ch[b][:], d.x[b]).then_inc(x_loaded[b], 16)
        for dst, src in ((offw, d.offw), (offb, d.offb), (base, d.base), (gmat, d.gmat)):
            sp.dma_start(dst[:], src).then_inc(consts, 16)
        sp.wait_ge(init, 1)
        for i in range(IMAGES):
            for row in (i * TROWS, (i + 1) * TROWS - P):
                sp.dma_start(d.table[row:row + P, :], zero[:]).then_inc(edges, 16)
        sp.wait_ge(edges, 2 * IMAGES * 16)
        for b in range(IMAGES):
            if b + SLOTS < IMAGES:
                sp.wait_ge(x_read, b + 1)
                sp.dma_start(x_ch[b % SLOTS][:], d.x[b + SLOTS]).then_inc(x_loaded[b % SLOTS], 16)
            sp.wait_ge(tr_free, (b + 1) * GROUPS)
            for c, off in enumerate(CORNERS):
                row = b * TROWS + MARGIN - off
                dst = d.table[row:row + PADPIX, c * P:(c + 1) * P]
                sp.dma_start(dst.rearrange("(i p) c -> p i c", p=P), pix[b % SLOTS][:]).then_inc(tables[b % SLOTS], 16)
        for s in range(SLOTS):
            sp.wait_ge(tables[s], IMAGES // SLOTS * 64)

    @block.vector
    def _(dve):
        v = nc.vector
        v.memset(zero[:], 0.0).then_inc(init, 1)
        v.memset(xpad[:], 0.0).then_inc(init, 1)
        for h in range(2):
            v.memset(ps_conv[h][:], 0.0).then_inc(init, 1)
        dve.wait_ge(init, 4)
        dve.wait_ge(consts, 64)
        with dve.Fori(0, IMAGES // SLOTS) as i:
            for s in range(SLOTS):
                b = i * SLOTS + s
                st = Steps(dve, dv, b * DVE_STEPS)
                dve.wait_ge(x_loaded[s], (i + 1) * 16)
                for j in range(8):
                    last = v.bn_stats(bn[:, j, :], x_ch[s][:, j * 512:(j + 1) * 512])
                st.link(last)
                dve.sem_inc(summed, 1)
                st.link(v.bn_aggr(agg[:], bn[:].rearrange("p a b -> p (a b)")))
                v.tensor_copy(gs[:, 0:1], agg[:, 0:1]).then_inc(stat_ready, 1)
                dve.wait_ge(group_ready, 2 * b + 1)
                st.link(v.tensor_copy(gs[:, 1:2], ps_g[:, 0:1]))
                st.link(v.tensor_tensor(gs[:, 2:3], agg[:, 0:1], gs[:, 1:2], ALU.subtract))
                st.link(v.tensor_tensor(gs[:, 2:3], gs[:, 2:3], gs[:, 2:3], ALU.mult))
                v.tensor_tensor(gs[:, 3:4], gs[:, 2:3], agg[:, 1:2], ALU.add).then_inc(stat_ready, 1)
                dve.wait_ge(group_ready, 2 * b + 2)
                st.link(v.tensor_scalar(gs[:, 4:5], ps_g[:, 1:2], 1e-5, None, ALU.add))
                rsqrt(nc, st, gs[:, 5:6], gs[:, 4:5], gs[:, 6:7], gs[:, 7:8])
                dve.wait_ge(tr_full, b * GROUPS)
                v.tensor_scalar(interior[:, 1:SIDE + 1, 1:SIDE + 1], x_ch[s][:].rearrange("p (y x) -> p y x", x=SIDE),
                                gs[:, 1:2], gs[:, 5:6], ALU.subtract, ALU.mult).then_inc(padded, 1)
                dve.wait_ge(padded, b + 1)
                dve.sem_inc(x_read, 1)
                for h in range(2):
                    dve.wait_ge(om_full, 2 * b + h + 1)
                    src = ps_om[:, h, :].rearrange("p (t j c) -> p j t c", t=4, c=32)[:, :, :, 0:OUTS]
                    dst = om[:, 16 * h:16 * h + 16, :].rearrange("p (j t) c -> p j t c", t=4)
                    v.tensor_copy(dst, src).then_inc(om_read, 1)
                dve.wait_ge(om_read, 2 * b + 2)
                py, px, fy, fx, t0, mask = [q[:] for q in pos]
                for q, axis in ((py, 0), (px, 1)):
                    st.link(v.tensor_tensor(q, om[:, :, axis:18:2], base[:, axis], ALU.add))
                    st.link(v.tensor_scalar(q, q, 0.0, SIDE + 1.0, ALU.max, ALU.min))
                for q, f in ((py, fy), (px, fx)):
                    st.link(v.tensor_scalar(f, q, MAGIC, MAGIC, ALU.add, ALU.subtract))
                    st.link(v.tensor_tensor(t0, f, q, ALU.is_gt))
                    st.link(v.tensor_tensor(f, f, t0, ALU.subtract))
                    st.link(v.tensor_tensor(q, q, f, ALU.subtract))
                flat = lambda q: q.rearrange("p t k -> p (t k)")
                st.link(v.scalar_tensor_tensor(out=t0, in0=fy, scalar=float(PADW), in1=fx, op0=ALU.mult, op1=ALU.add))
                idx = r.idx[:, bass.ds(b * (TILES * TAPS), TILES * TAPS)]
                st.link(v.tensor_scalar(idx, flat(t0), r.image_row[:, bass.ds(b, 1)], None, ALU.add))
                dve.wait_ge(sig, b + 1)
                wt = r.wts[:, bass.ds(b * TILES, TILES)]
                st.link(v.tensor_scalar(fy, py, -1.0, 1.0, ALU.mult, ALU.add))
                st.link(v.tensor_tensor(fy, fy, mask, ALU.mult))
                st.link(v.tensor_tensor(py, py, mask, ALU.mult))
                v.tensor_tensor(wt[:, :, :, 1], fy, px, ALU.mult)
                v.tensor_tensor(wt[:, :, :, 3], py, px, ALU.mult)
                st.link(v.tensor_scalar(fx, px, -1.0, 1.0, ALU.mult, ALU.add))
                v.tensor_tensor(wt[:, :, :, 0], fy, fx, ALU.mult)
                st.link(v.tensor_tensor(wt[:, :, :, 2], py, fx, ALU.mult))
                assert st.n == DVE_STEPS, st.n

    @block.scalar
    def _(act):
        act.wait_ge(consts, 64)
        with act.Fori(0, IMAGES // SLOTS) as i:
            for s in range(SLOTS):
                b = i * SLOTS + s
                for h in range(2):
                    act.wait_ge(conv_full, 2 * b + h + 1)
                    act.wait_ge(om_full, 2 * b)
                    nc.scalar.activation(om_ch[h][:], ps_conv[h][:], ACT.Identity, bias=offb[:]).then_inc(conv_read, 1)
                for g in range(GROUPS):
                    act.wait_ge(tr_full, b * GROUPS + g + 1)
                    if g == 0:
                        act.wait_ge(tables[s], i * 64)
                    nc.scalar.copy(pix[s][:, 4 * g:4 * g + 4, :].rearrange("p a c -> p (a c)"), ps_t[:, g % 2, :]).then_inc(tr_free, 1)
                act.wait_ge(om_read, 2 * b + 2)
                nc.scalar.activation(pos[5][:], om[:, :, 2 * TAPS:], ACT.Sigmoid).then_inc(sig, 1)

    @block.tensor
    def _(pe):
        pe.wait_ge(consts, 64)
        pe.wait_ge(init, 4)
        with pe.Fori(0, IMAGES) as b:
            for k, col in ((0, 0), (1, 3)):
                pe.wait_ge(stat_ready, 2 * b + k + 1)
                nc.tensor.matmul(ps_g[:, k:k + 1], gmat[:], gs[:, col:col + 1], start=True, stop=True).then_inc(group_ready, 1)
            pe.wait_ge(padded, b + 1)
            pe.wait_ge(conv_read, 2 * b)
            for h in range(2):
                for k in range(TAPS):
                    ky, kx = divmod(k, 3)
                    for j in range(4):
                        y = 8 * (4 * h + j) + ky
                        last = nc.tensor.matmul(ps_conv[h][32 * j:32 * j + OUTS, :], offw[:, k, :], interior[:, y:y + 8, kx:kx + SIDE],
                                                start=(k == 0), stop=(k == TAPS - 1))
                last.then_inc(conv_full, 1)
            for h in range(2):
                pe.wait_ge(conv_read, 2 * b + h + 1)
                pe.wait_ge(om_read, 2 * b)
                for t in range(4):
                    last = nc.tensor.transpose(ps_om[:, h, t * P:(t + 1) * P], om_ch[h][:, t * P:(t + 1) * P], r.ident[:])
                last.then_inc(om_full, 1)
            for g in range(GROUPS):
                if g >= 2:
                    pe.wait_ge(tr_free, b * GROUPS + g - 1)
                elif g == 0:
                    pe.wait_ge(tr_free, b * GROUPS)
                for j in range(4):
                    i = 4 * g + j
                    last = nc.tensor.transpose(ps_t[:, g % 2, j * P:(j + 1) * P], xpad[:, i * P:(i + 1) * P], r.ident[:])
                last.then_inc(tr_full, 1)


def token_tiles(t, n, w=2):
    return t[bass.ds(n * (w * P), w * P), :].rearrange("(t p) c -> p t c", p=P)


def cosine_ring(nc, st, q, cum, c):
    v = nc.vector
    st.inc(v.tensor_tensor(q[:, :, 1], c[:, :, 0], c[:, :, 1], ALU.mult))
    st.link(v.tensor_tensor(cum[:, :, 0], c[:, :, 1], c[:, :, 2], ALU.mult))
    for j in range(2, HD):
        st.inc(v.tensor_tensor(q[:, :, j], q[:, :, j - 1], c[:, :, j], ALU.mult))
        if j + 1 < HD:
            dst = q[:, :, 0] if j + 1 == HD - 1 else cum[:, :, (j + 1) % 2]
            st.inc(v.tensor_tensor(dst, cum[:, :, j % 2], c[:, :, j + 1], ALU.mult))
        st.wait()


def theta_phases(r, w):
    return r.theta[:].rearrange("p (o c) -> p o c", o=1).to_broadcast([P, w, P])


def store_ring(sp, d, q, row, t, stored):
    dst = d.q[:, bass.ds(row, P), :].rearrange("g p c -> p g c")
    sp.dma_start(dst, q[:, t, :].rearrange("p (g c) -> p g c", g=QUADS)).then_inc(stored, 16)


LEAD, LAG = 20, 16


def stage_conv_first(nc, d, r, stack):
    sb = lambda n, s, t=F32: stack.enter_context(nc.sbuf_tensor(n, s, t))
    sem = lambda n: stack.enter_context(nc.semaphore(n))
    W = 4
    ROUNDS = 2 * LEAD // W
    GROUPS = ((0, 4), (4, 8), (8, 9))
    NG = len(GROUPS)
    FINISH_STEPS = 47
    idx_st, w_st = [sb(f"cf_idx{j}", [P, TAPS], I32) for j in range(W)], [sb(f"cf_w{j}", [P, TAPS, 4]) for j in range(W)]
    corners = [sb(f"cf_corners{j}", [P, TAPS, 512]) for j in range(W)]
    val, val_t = [[sb(f"cf_val{j}_{c}", [P, TAPS, P]) for c in range(2)] for j in range(2)], [sb(f"cf_val_t{j}", [P, TAPS * P]) for j in range(2)]
    xt, t1, xn, ph, tmp, tmp2, tmp3, q = (sb("cf_" + n, [P, W, P]) for n in ("xt", "t1", "xn", "ph", "tmp", "tmp2", "tmp3", "q"))
    cum, stat = sb("cf_cum", [P, W * HEADS, 2]), sb("cf_stat", [P, 4, W])
    ps_t = [stack.enter_context(nc.psum_tensor(f"cf_ps_t{i}", [P, 512], F32)) for i in range(2)]
    ps_y = stack.enter_context(nc.psum_tensor("cf_ps_y", [P, W * P], F32))
    dv, idx_ready, w_ready, gathering, act_val, val_ready, tr_full, tr_free, prod_done, x_in, t1_ready, q_ready, stored = (
        sem("cf_" + n) for n in ("dve", "idx_ready", "w_ready", "gathering", "act_val", "val_ready", "tr_full", "tr_free",
                                 "prod_done", "x_in", "t1_ready", "q_ready", "stored"))
    gathered = [sem(f"cf_gathered{j}") for j in range(W)]
    PER_ROUND = (1 + W) * 16
    block = stack.enter_context(nc.Block())

    @block.sync
    def _(sp):
        with sp.Fori(0, ROUNDS) as i:
            sp.wait_ge(t1_ready, i)
            sp.dma_start(xt[:], token_tiles(d.x_tok, i, W)).then_inc(x_in, 16)
            sp.wait_ge(t1_ready, i + 1)
            sp.dma_start(token_tiles(d.t1, i, W), t1[:]).then_inc(stored, 16)
            sp.wait_ge(q_ready, i + 1)
            for t in range(W):
                store_ring(sp, d, q, i * (W * P) + t * P, t, stored)
        sp.wait_ge(stored, ROUNDS * PER_ROUND)

    @block.gpsimd
    def _(pool):
        with pool.Fori(0, ROUNDS) as i:
            for j in range(W):
                pool.wait_ge(idx_ready, i * W + j + 1)
                pool.sem_inc(gathering, 1)
                for k in range(TAPS):
                    pool.indirect_dma_start(corners[j][:, k, :], None, d.table,
                                            bass.IndirectOffsetOnAxis(idx_st[j][:, k:k + 1], 0)).then_inc(gathered[j], 16)

    @block.vector
    def _(dve):
        v = nc.vector

        def stage(tile, j):
            v.tensor_copy(w_st[j][:].rearrange("p k c -> p (k c)"),
                          r.wts[:, bass.ds(tile, 1)].rearrange("p o k c -> p (o k c)")).then_inc(w_ready, 1)
            v.tensor_copy(idx_st[j][:], r.idx[:, bass.ds(tile * TAPS, TAPS)]).then_inc(idx_ready, 1)

        for j in range(W):
            stage(j, j)
        def sample(i, j, st):
            n = i * W + j
            dve.wait_ge(gathered[j], (i + 1) * (16 * TAPS))
            dve.wait_ge(tr_full, (n + 1) * NG)
            for c in (1, 2, 3):
                for k in range(TAPS):
                    src, wt, dst = corners[j][:, k, c * P:(c + 1) * P], w_st[j][:, k, c:c + 1], val[j % 2][1][:, k, :]
                    if c == 1:
                        last = v.tensor_scalar(dst, src, wt, None, ALU.mult)
                    else:
                        last = v.scalar_tensor_tensor(out=dst, in0=src, scalar=wt, in1=dst, op0=ALU.mult, op1=ALU.add)
                if c < 3:
                    st.link(last)
            last.then_inc(val_ready, 1)
            dve.wait_ge(val_ready, n + 1)
            dve.wait_ge(act_val, n + 1)
            stage((n + W) % (2 * PAIRS), j)

        def finish(i, st):
            dve.wait_ge(prod_done, (i + 1) * W)
            dve.wait_ge(x_in, (i + 1) * 16)
            dve.wait_ge(stored, i * PER_ROUND)
            v.tensor_tensor(t1[:].rearrange("p t c -> p (t c)"), ps_y[:], xt[:].rearrange("p t c -> p (t c)"), ALU.add).then_inc(t1_ready, 1)
            dve.wait_ge(t1_ready, i + 1)
            n0 = st.n
            layer_norm(nc, st, xn[:], t1[:], tmp[:], stat, W, P, 1e-5)
            st.link(v.tensor_tensor(ph[:], xn[:], theta_phases(r, W), ALU.add))
            cosine(nc, st, ph[:], tmp[:], tmp2[:], tmp3[:])
            heads = lambda x: x[:].rearrange("p t (h d) -> p (t h) d", d=HD)
            cosine_ring(nc, st, heads(q), cum, heads(ph))
            dve.sem_inc(q_ready, 1)
            assert st.n - n0 == FINISH_STEPS, st.n - n0

        st = Steps(dve, dv)
        for j in range(W):
            sample(0, j, st)
        with dve.Fori(1, ROUNDS) as i:
            st = Steps(dve, dv, (i - 1) * (2 * W + FINISH_STEPS) + 2 * W)
            sample(i, 0, st)
            finish(i - 1, st)
            for j in range(1, W):
                sample(i, j, st)
        finish(ROUNDS - 1, Steps(dve, dv, (ROUNDS - 1) * (2 * W + FINISH_STEPS) + 2 * W))

    @block.scalar
    def _(act):
        def corner(i, j):
            n = i * W + j
            act.wait_ge(gathered[j], (i + 1) * (16 * TAPS))
            act.wait_ge(w_ready, n + 1)
            act.wait_ge(tr_full, (n + 1) * NG)
            for k in range(TAPS):
                last = nc.scalar.activation(val[j % 2][0][:, k, :], corners[j][:, k, 0:P], ACT.Copy, scale=w_st[j][:, k, 0:1])
            last.then_inc(act_val, 1)

        def copy_turned(i, j):
            n = i * W + j
            if j >= 2:
                act.wait_ge(prod_done, n - 1)
            else:
                act.wait_ge(prod_done, i * W)
            for g, (g0, g1) in enumerate(GROUPS):
                act.wait_ge(tr_full, (n + 2) * NG + g + 1)
                nc.scalar.copy(val_t[j % 2][:, g0 * P:g1 * P], ps_t[(j * NG + g) % 2][:, 0:(g1 - g0) * P]).then_inc(tr_free, 1)

        with act.Fori(0, ROUNDS) as i:
            corner(i, 0)
            for j in range(1, W):
                corner(i, j)
                copy_turned(i, j - 1)
            copy_turned(i, W - 1)

    @block.tensor
    def _(pe):
        pe.sem_inc(tr_full, 2 * NG)
        with pe.Fori(0, ROUNDS) as i:
            for j in range(W):
                n = i * W + j
                pe.wait_ge(val_ready, n + 1)
                pe.wait_ge(act_val, n + 1)
                for g, (g0, g1) in enumerate(GROUPS):
                    at = j * NG + g
                    if at >= 2:
                        pe.wait_ge(tr_free, i * (W * NG) + (at - 1))
                    elif at == 0:
                        pe.wait_ge(tr_free, i * (W * NG))
                    for k in range(g0, g1):
                        for c in range(2):
                            last = nc.tensor.matmul(ps_t[at % 2][:, (k - g0) * P:(k - g0 + 1) * P], val[j % 2][c][:, k, :], r.ident[:],
                                                    start=(c == 0), stop=(c == 1))
                    last.then_inc(tr_full, 1)
                pe.wait_ge(tr_free, (n + 1) * NG)
                if j == 0:
                    pe.wait_ge(t1_ready, i)
                for k in range(TAPS):
                    last = nc.tensor.matmul(ps_y[:, j * P:(j + 1) * P], val_t[j % 2][:, k * P:(k + 1) * P], r.dcnw[:, k, :],
                                            start=(k == 0), stop=(k == TAPS - 1))
                last.then_inc(prod_done, 1)


class ConvStep:

    def __init__(self, nc, d, r, stack, misc):
        sb = lambda n, s, t=F32: stack.enter_context(nc.sbuf_tensor(n, s, t))
        sem = lambda n: stack.enter_context(nc.semaphore(n))
        self.nc, self.d, self.r, self.misc = nc, d, r, misc
        self.idx_st = [sb(f"idx_st{s}", [P, TAPS], I32) for s in range(2)]
        self.w_st = [sb(f"w_st{s}", [P, TAPS, 4]) for s in range(2)]
        self.corners = [sb(f"corners{s}", [P, TAPS, 512]) for s in range(2)]
        self.val = [sb(f"val{s}", [P, TAPS, P]) for s in range(2)]
        self.val_t = sb("val_t", [P, TAPS * P])
        self.xt = sb("xt", [P, 2, P])
        self.t1 = sb("t1_out", [P, 2, P])
        self.xn, self.ph, self.tmp, self.tmp2, self.tmp3 = (sb(n, [P, 2, P]) for n in ("xn", "ph", "ctmp", "ctmp2", "ctmp3"))
        self.cum = sb("cum", [P, 2 * HEADS, 2])
        self.q = sb("q_out", [P, 2, P])
        self.stat = sb("cstat", [P, 4, 2])
        self.dv, self.idx_ready, self.w_copied = sem("conv_dve"), sem("idx_ready"), sem("w_copied")
        self.gathered = [sem(f"gathered{s}") for s in range(2)]
        self.gathering, self.val_ready, self.x_in, self.t1_ready, self.q_ready, self.stored = (
            sem(n) for n in ("gathering", "val_ready", "x_in", "t1_ready", "q_ready", "conv_stored"))

    def load_sp(self, sp, n):
        sp.wait_ge(self.t1_ready, n - LEAD)
        sp.dma_start(self.xt[:], token_tiles(self.d.x_tok, n)).then_inc(self.x_in, 16)

    def store_sp(self, sp, n):
        sp.wait_ge(self.t1_ready, n - LEAD + 1)
        sp.dma_start(token_tiles(self.d.t1, n), self.t1[:]).then_inc(self.stored, 16)
        sp.wait_ge(self.q_ready, n - LEAD + 1)
        for t in range(2):
            store_ring(sp, self.d, self.q, n * 256 + t * P, t, self.stored)

    def gather_pool(self, pool, n, s, taps):
        for k in taps:
            if k == 0:
                pool.wait_ge(self.idx_ready, 2 * (n - LEAD) + s + 1)
                pool.wait_ge(self.val_ready, 2 * (n - LEAD) + s + 1)
                pool.sem_inc(self.gathering, 1)
            pool.indirect_dma_start(self.corners[s][:, k, :], None, self.d.table,
                                    bass.IndirectOffsetOnAxis(self.idx_st[s][:, k:k + 1], 0)).then_inc(self.gathered[s], 16)

    STEPS = 53

    def stage_dve(self, dve, n, s):
        v, r = self.nc.vector, self.r
        v.tensor_copy(self.w_st[s][:].rearrange("p k c -> p (k c)"),
                      r.wts[:, bass.ds(2 * n + s, 1)].rearrange("p o k c -> p (o k c)")).then_inc(self.w_copied, 1)
        v.tensor_copy(self.idx_st[s][:], r.idx[:, bass.ds((2 * n + s) * TAPS, TAPS)]).then_inc(self.idx_ready, 1)

    def sample_dve(self, dve, n, s, st):
        v = self.nc.vector
        dve.wait_ge(self.gathered[s], (n - LEAD + 1) * (16 * TAPS))
        dve.wait_ge(self.w_copied, 2 * (n - LEAD) + s + 1)
        g, val, w = self.corners[s], self.val[s], self.w_st[s]
        for c in range(4):
            for k in range(TAPS):
                src, wt = g[:, k, c * P:(c + 1) * P], w[:, k, c:c + 1]
                if c == 0:
                    last = v.tensor_scalar(val[:, k, :], src, wt, None, ALU.mult)
                else:
                    last = v.scalar_tensor_tensor(out=val[:, k, :], in0=src, scalar=wt, in1=val[:, k, :],
                                                  op0=ALU.mult, op1=ALU.add)
            if c < 3:
                st.link(last)
        last.then_inc(self.val_ready, 1)
        dve.wait_ge(self.val_ready, 2 * (n - LEAD) + s + 3)
        self.stage_dve(dve, (n + 1) % PAIRS, s)

    def product_dve(self, dve, n, s):
        v, m = self.nc.vector, self.misc
        for g0, g1 in self.GROUPS:
            m.dve_take(dve)
            m.dve_give(v.tensor_copy(self.val_t[:, g0 * P:g1 * P], m.bank[:, 0:(g1 - g0) * P]))
        m.dve_take(dve)
        if s == 0:
            dve.wait_ge(self.x_in, (n - LEAD + 1) * 16)
            dve.wait_ge(self.stored, (n - LEAD) * 48)
        m.dve_give(v.tensor_tensor(self.t1[:, s, :], m.bank[:, 0:P], self.xt[:, s, :], ALU.add))

    def ring_dve(self, dve, n, st):
        nc, r, m = self.nc, self.r, self.misc
        v = nc.vector
        m.dve_wait_given(dve)
        dve.sem_inc(self.t1_ready, 1)
        layer_norm(nc, st, self.xn[:], self.t1[:], self.tmp[:], self.stat, 2, P, 1e-5)
        st.link(v.tensor_tensor(self.ph[:], self.xn[:], theta_phases(r, 2), ALU.add))
        cosine(nc, st, self.ph[:], self.tmp[:], self.tmp2[:], self.tmp3[:])
        heads = lambda x: x[:].rearrange("p t (h d) -> p (t h) d", d=HD)
        cosine_ring(nc, st, heads(self.q), self.cum, heads(self.ph))
        dve.sem_inc(self.q_ready, 1)

    GROUPS = ((0, 4), (4, 8), (8, 9))

    def transposes_pe(self, pe, n, s, g):
        m = self.misc
        if g == 0:
            pe.wait_ge(self.val_ready, 2 * (n - LEAD) + s + 3)
        g0, g1 = self.GROUPS[g]
        m.pe_take(pe)
        for k in range(g0, g1):
            last = self.nc.tensor.transpose(m.bank[:, (k - g0) * P:(k - g0 + 1) * P], self.val[s][:, k, :], self.r.ident[:])
        m.pe_give(last)

    def product_pe(self, pe, part):
        m = self.misc
        if part == 0:
            m.pe_take(pe)
        for k in range(3 * part, 3 * part + 3):
            last = self.nc.tensor.matmul(m.bank[:, 0:P], self.val_t[:, k * P:(k + 1) * P], self.r.dcnw[:, k, :],
                                         start=(k == 0), stop=(k == TAPS - 1))
        if part == 2:
            m.pe_give(last)

    def items_pe(self, pe, n, s):
        return ([lambda g=g: self.transposes_pe(pe, n, s, g) for g in range(3)]
                + [lambda i=i: self.product_pe(pe, i) for i in range(3)])


class Misc:

    def __init__(self, bank, full, free):
        self.bank, self.full, self.free = bank, full, free
        self.base, self.p, self.d = 0, 0, 0

    def start(self, base):
        self.base, self.p, self.d = base, 0, 0

    def pe_take(self, pe):
        pe.wait_ge(self.free, self.base + (self.p + 1))

    def pe_give(self, ins):
        self.p += 1
        ins.then_inc(self.full, 1)

    def dve_take(self, dve):
        dve.wait_ge(self.full, self.base + (self.d + 1))

    def dve_give(self, ins):
        self.d += 1
        ins.then_inc(self.free, 1)

    def dve_wait_given(self, dve):
        dve.wait_ge(self.free, self.base + (self.d + 1))


class AttnStep:

    SC, NE = 3, 8
    STEPS = 2 * TILES * 2
    UNIT = TILES
    EVERY, SPLITS = 4, 14
    E1 = HD + 1
    PV_START = NE // 2

    def __init__(self, nc, d, r, stack, misc):
        sb = lambda n, s, t=F32: stack.enter_context(nc.sbuf_tensor(n, s, t))
        sem = lambda n: stack.enter_context(nc.semaphore(n))
        self.nc, self.d, self.r, self.misc = nc, d, r, misc
        self.qn = sb("qn", [P, TILES, 4 * HD])
        self.wa, self.wb = (sb(n, [P, 8, 4, 4, HD], F16) for n in ("wa", "wb"))
        self.a_next, self.a = (sb(n, [P, TOK], F16) for n in ("a_next", "a_cur"))
        self.b = sb("b_two_quads", [P, 2 * TOK], F16)
        self.v_next, self.v = (sb(n, [P, TILES, 4, HD + 1]) for n in ("v_next", "v_cur"))
        self.vb_next, self.vb = (sb(n, [P, TILES // self.EVERY, 4, 3 * self.E1], BF16) for n in ("vb_next", "vb_cur"))
        self.vh_next, self.vh = (sb(n, [P, TILES // self.EVERY, 4, 2 * self.E1], F16) for n in ("vh_next", "vh_cur"))
        self.v_rest, self.sums = sb("v_rest", [P, 2, 4, HD]), sb("ctx_sums", [P, 16, self.E1])
        self.e_low = [sb(f"e_low{i}", [P, 4, CHUNK], F16) for i in range(2)]
        self.bst = [sb(f"b_unit{s}", [P, 4, CHUNK], F16) for s in range(2)]
        self.e = [sb(f"e{i}", [P, 2, CHUNK]) for i in range(self.NE)]
        self.acc_sb, self.rs = sb("acc_sb", [P, CHUNK]), sb("rs", [P, 16])
        self.ctx_t = [sb(f"ctx_t{s}", [P, 4, 4 * HD]) for s in range(2)]
        self.sc = [stack.enter_context(nc.psum_tensor(f"sc{i}", [P, 2, CHUNK], F32)) for i in range(self.SC)]
        self.acc = stack.enter_context(nc.psum_tensor("acc", [P, CHUNK], F32))
        (self.q_in, self.staged, self.a_switched, self.v_switched, self.units_ready, self.sc_ready, self.exp_done,
         self.pv_done, self.acc_read, self.dv_stage, self.dv_finish, self.w_ready, self.ctx_ready, self.init,
         self.low_ready, self.low_used) = (sem(n) for n in (
             "q_in", "q_staged", "a_switched", "v_switched", "units_ready", "sc_ready", "exp_done",
             "pv_done", "acc_read", "stage_dve", "finish_dve", "w_ready", "ctx_ready", "attn_init",
             "low_ready", "low_used"))
        self.ctx_stored = [sem(f"ctx_stored{s}") for s in range(2)]

    def init_dve(self, dve):
        v = self.nc.vector
        v.memset(self.acc[:], 1.0).then_inc(self.init, 1)
        v.memset(self.v_next[:], 1.0).then_inc(self.init, 1)
        for s in range(2):
            v.memset(self.bst[s][:], 0.0).then_inc(self.init, 1)
        for parts in (self.vb_next, self.vh_next):
            v.memset(parts[:], 0.0).then_inc(self.init, 1)
        dve.wait_ge(self.init, 6)
        for parts in (self.vb_next, self.vh_next):
            v.memset(parts[:, :, :, HD:HD + 1], 1.0).then_inc(self.init, 1)
        dve.wait_ge(self.init, 8)

    def load_q(self, sp, qd):
        sp.wait_ge(self.staged, 4 * qd)
        src = self.d.q[bass.ds(qd % QUADS, 1), bass.ds((qd // QUADS) * TOK, TOK), :].rearrange("g (t p) c -> p (g t) c", p=P)
        sp.dma_start(self.qn[:], src).then_inc(self.q_in, 16)

    def stage_dve(self, dve, qd, p):
        v, m = self.nc.vector, self.misc
        st = Steps(dve, self.dv_stage, (4 * qd + p) * 6)
        dve.wait_ge(self.a_switched, qd)
        dve.wait_ge(self.v_switched, qd)
        dve.wait_ge(self.q_in, (qd + 1) * 16)
        q = self.qn[:, bass.ds(p * 8, 8), :].rearrange("p t (h d) -> p (t h) d", d=HD)
        wa = self.wa[:].rearrange("p t h v d -> p (t h) v d")
        wb = self.wb[:].rearrange("p t h v d -> p (t h) v d")
        vn = self.v_next[:, bass.ds(p * 8, 8)].rearrange("p t h e -> p (t h) e")
        two = lambda parts, x: parts[:, bass.ds(p * 2, 2), :, x * self.E1:x * self.E1 + HD]
        q2 = self.qn[:, bass.ds(p * 8, 8), :].rearrange("p (a f) c -> p a f c", f=self.EVERY)[:, :, 0, :].rearrange("p a (h d) -> p a h d", d=HD)
        st.link(v.tensor_copy(two(self.vb_next, 0), q2))
        st.link(v.tensor_tensor(self.v_rest[:], q2, two(self.vb_next, 0), ALU.subtract))
        st.link(v.tensor_copy(two(self.vb_next, 1), self.v_rest[:]))
        st.link(v.tensor_tensor(self.v_rest[:], self.v_rest[:], two(self.vb_next, 1), ALU.subtract))
        v.tensor_copy(two(self.vb_next, 2), self.v_rest[:])
        v.tensor_copy(vn[:, :, 0:HD], q)
        st.link(v.tensor_copy(wa[:, :, 0, :], q))
        v.tensor_tensor(wa[:, :, 1, :], q, wa[:, :, 0, :], ALU.subtract).then_inc(self.staged, 1)
        dve.wait_ge(self.staged, 4 * qd + p + 1)
        v.tensor_copy(wa[:, :, 2:4, :], wa[:, :, 0:2, :])
        v.tensor_copy(wb[:, :, 0:2, :], wa[:, :, 0:2, :])
        v.tensor_copy(wb[:, :, 2, :], wa[:, :, 1, :])
        st.link(v.tensor_copy(wb[:, :, 3, :], wa[:, :, 0, :]))
        dve.sem_inc(self.w_ready, 1)
        for x in range(2):
            v.tensor_copy(two(self.vh_next, x), self.wa[:, 0::self.EVERY, :, x, :])
        assert st.n == 6
        m.dve_take(dve)
        m.dve_give(v.tensor_copy(self.a_next[:, bass.ds(p * 1024, 1024)], m.bank[:].bitcast(F16)))
        m.dve_take(dve)
        m.dve_give(v.tensor_copy(self.b[:, bass.ds((qd % 2) * TOK + p * 1024, 1024)], m.bank[:].bitcast(F16)))
        m.dve_wait_given(dve)

    def stage_pe(self, pe, qd, p, k):
        m = self.misc
        m.pe_take(pe)
        pe.wait_ge(self.w_ready, 4 * qd + p + 1)
        w = (self.wa, self.wb)[k][:].rearrange("p t h v d -> p t (h v d)")
        out = m.bank[:].bitcast(F16)
        for t in range(8):
            last = self.nc.tensor.transpose(out[:, t * P:(t + 1) * P], w[:, t, :], self.r.ident16[:])
        m.pe_give(last)

    def switch_dve(self, dve, qd):
        v = self.nc.vector
        if not isinstance(qd, int) or qd > 0:
            dve.wait_ge(self.sc_ready, qd * (QPAIRS * self.STEPS))
        v.tensor_copy(self.a[:], self.a_next[:]).then_inc(self.a_switched, 1)
        dve.wait_ge(self.pv_done, qd * (UNITS * self.UNIT) + self.PV_START)
        v.tensor_copy(self.vb[:], self.vb_next[:])
        v.tensor_copy(self.vh[:], self.vh_next[:])
        v.tensor_copy(self.v[:], self.v_next[:]).then_inc(self.v_switched, 1)

    def unit_dve(self, s, u):
        v = self.nc.vector
        col = ((u // UNITS) % 2) * TOK + (u % UNITS) * CHUNK
        for h in range(4):
            rows = slice(32 * h, 32 * h + 32)
            last = v.tensor_copy(self.bst[s][rows, h, :], self.b[rows, bass.ds(col, CHUNK)])
        last.then_inc(self.units_ready, 1)

    def finish_dve(self, dve, u, n, s, next_unit=None):
        v, m = self.nc.vector, self.misc
        dve.wait_ge(self.pv_done, u * self.UNIT + self.PV_START)
        v.tensor_copy(self.acc_sb[:], self.acc[:]).then_inc(self.acc_read, 1)
        if next_unit is not None:
            self.unit_dve(s, next_unit)
        m.dve_take(dve)
        o = m.bank[:].rearrange("p (a e) -> p a e", e=32)
        st, E1 = Steps(dve, self.dv_finish, u * 3), self.E1
        st.link(v.tensor_copy(self.sums[:], o[:, :, 0:E1]))
        for x in (1, 2):
            ins = v.tensor_tensor(self.sums[:], self.sums[:], o[:, :, x * E1:(x + 1) * E1], ALU.add)
            if x == 1:
                st.link(ins)
            else:
                m.dve_give(ins)
        m.dve_wait_given(dve)
        st.link(v.reciprocal(self.rs[:].rearrange("p (a o) -> p a o", o=1), self.sums[:, :, HD:HD + 1]))
        dve.wait_ge(self.ctx_stored[s], n * 16)
        ctx = self.ctx_t[s][:].rearrange("p t (h d) -> p (t h) d", d=HD)
        v.tensor_tensor(ctx, self.sums[:, :, 0:HD], bcast(self.rs[:], HD), ALU.mult).then_inc(self.ctx_ready, 1)

    def finish_pe(self, pe, u):
        m = self.misc
        m.pe_take(pe)
        pe.wait_ge(self.acc_read, u + 1)
        for t in range(4):
            last = self.nc.tensor.transpose(m.bank[:, t * P:(t + 1) * P], self.acc_sb[:, t * P:(t + 1) * P], self.r.ident[:])
        m.pe_give(last)

    def store_ctx(self, sp, u, s):
        sp.wait_ge(self.ctx_ready, u + 2)
        qd, c = u // UNITS, u % UNITS
        dst = self.d.ctx[bass.ds((qd // QUADS) * TOK + c * CHUNK, CHUNK), bass.ds((qd % QUADS) * 32, 32)]
        sp.dma_start(dst.rearrange("(t p) c -> p t c", p=P), self.ctx_t[s][:]).then_inc(self.ctx_stored[s], 16)

    def scores(self, pe, k, s):
        t, hp = divmod(k % (self.STEPS // 2), 2)
        for i in range(2):
            last = self.nc.tensor.matmul(self.sc[k % self.SC][:, i, :], self.a[:, t * P:(t + 1) * P],
                                         self.bst[s][:, 2 * hp + i, :], start=True, stop=True)
        last.then_inc(self.sc_ready, 1)

    def values(self, pe, g, n):
        s, t = divmod(g, self.UNIT)
        if t == 0:
            pe.wait_ge(self.acc_read, 2 * n + s + 1)
            if s == 0:
                pe.wait_ge(self.v_switched, n // QPAIRS + 1)
        for h in range(4):
            e = self.e[(2 * g + h // 2) % self.NE][:, h % 2, :]
            if self.split(t):
                last = self.nc.tensor.matmul(self.acc[32 * h:32 * h + 3 * self.E1, :], self.vb[:, t // self.EVERY, h, :],
                                             e.bitcast(BF16)[:, 1::2], start=(t == 0), stop=False)
            else:
                last = self.nc.tensor.matmul(self.acc[32 * h:32 * h + self.E1, :], self.v[:, t, h, :], e,
                                             start=False, stop=(t == self.UNIT - 1))
        last.then_inc(self.pv_done, 1)
        if self.split(t - self.EVERY):
            self.low_values(pe, s, t - self.EVERY, n)

    def split(self, t):
        return t % self.EVERY == 0 and 0 <= t < self.UNIT - self.EVERY

    def low_values(self, pe, s, t, n):
        m = s * (self.SPLITS // 2) + t // self.EVERY
        pe.wait_ge(self.low_ready, n * self.SPLITS + (m + 1))
        for h in range(4):
            last = self.nc.tensor.matmul(self.acc[32 * h:32 * h + 2 * self.E1, :], self.vh[:, t // self.EVERY, h, :],
                                         self.e_low[m % 2][:, h, :], start=False, stop=False)
        last.then_inc(self.low_used, 1)

    def split_pool(self, pool, n, m):
        k = self.STEPS // 2 * (m // (self.SPLITS // 2)) + 2 * self.EVERY * (m % (self.SPLITS // 2))
        pool.wait_ge(self.low_used, n * self.SPLITS + (m + 1))
        for i in range(2):
            pool.wait_ge(self.exp_done, n * self.STEPS + (k + i + 1 + self.SC))
            e = self.e[(k + i) % self.NE][:].rearrange("p h q -> p (h q)")
            last = self.nc.gpsimd.tensor_tensor(self.e_low[m % 2][:, 2 * i:2 * i + 2, :].rearrange("p h q -> p (h q)"), e,
                                                e.bitcast(BF16)[:, 1::2], ALU.subtract)
        last.then_inc(self.low_ready, 1)

    def first_scores(self, pe, n, a_need):
        pe.wait_ge(self.units_ready, 2 * n + 1)
        pe.wait_ge(self.a_switched, a_need)
        pe.wait_ge(self.exp_done, n * self.STEPS + 2)
        self.scores(pe, 0, 0)
        pe.wait_ge(self.exp_done, n * self.STEPS + 3)
        self.scores(pe, 1, 0)
        self.scores(pe, 2, 0)

    def pair_pe(self, pe, n, background, a_next_need):
        for k in range(3, self.STEPS):
            if k == self.STEPS // 2:
                pe.wait_ge(self.units_ready, 2 * n + 2)
            pe.wait_ge(self.exp_done, n * self.STEPS + (k + 1))
            self.scores(pe, k, k // (self.STEPS // 2))
            if k % 2 and k >= 5:
                self.values(pe, (k - 5) // 2, n)
            if k in background:
                background[k]()
        pe.wait_ge(self.exp_done, n * self.STEPS + (self.STEPS - 2 + self.SC))
        self.values(pe, 2 * self.UNIT - 2, n)
        self.first_scores(pe, n + 1, a_next_need)
        self.values(pe, 2 * self.UNIT - 1, n)

    def pair_act(self, act, n):
        base = n * self.STEPS
        for k in range(self.STEPS):
            act.wait_ge(self.sc_ready, base + (k + 1))
            if k % 2 == 0:
                act.wait_ge(self.pv_done, n * (2 * self.UNIT) + (k // 2 + 1))
                s, t = divmod(max(k // 2 - self.NE // 2, 0), self.UNIT)
                if k >= self.NE and self.split(t):
                    act.wait_ge(self.low_ready, n * self.SPLITS + (s * (self.SPLITS // 2) + t // self.EVERY + 1))
            self.nc.scalar.activation(self.e[k % self.NE][:], self.sc[k % self.SC][:], ACT.Exp,
                                      scale=1.0 / HD ** 0.5).then_inc(self.exp_done, 1)



def within(*buffers):
    free = [b[:].rearrange("p k c -> p (k c)") for b in buffers]

    def take(name, shape):
        size = int(np.prod(shape[1:]))
        i = next(i for i, b in enumerate(free) if b.shape[1] >= size)
        got, free[i] = free[i][0:shape[0], 0:size], free[i][:, size:]
        if len(shape) == 3:
            return got.rearrange("p (a b) -> p a b", a=shape[1])
        return got

    return take


class FfnStep:

    DVE_STEPS = 77

    def __init__(self, nc, d, r, stack, misc, w, first, room=None):
        def sb(n, s):
            if callable(room):
                return room(n, s)
            return room[n] if room and n in room else stack.enter_context(nc.sbuf_tensor(n + f"_{w}", s, F32))

        sem = lambda n: stack.enter_context(nc.semaphore(n + f"_{w}"))
        self.w, self.first = w, first
        self.chunks = max(1, 4 // w)
        self.items = 4 + 4 // self.chunks
        self.nc, self.d, self.r, self.misc = nc, d, r, misc
        self.t1, self.ctx, self.xn, self.x1, self.y, self.tmp, self.t2 = (
            sb("f_" + n, [P, w, P]) for n in ("t1", "ctx", "xn", "x1", "y", "tmp", "t2"))
        self.stat, self.ctx_t, self.zf = sb("f_stat", [P, 4, w]), sb("f_ctx_t", [P, w * P]), sb("f_zf", [P, w, HD + 1])
        self.z = [sb(f"f_z{i}", [P, w, HD]) for i in range(4)]
        self.zf_t, self.h_t = sb("f_zf_t", [HD + 1, w * P]), sb("f_h_t", [P, 4, w * P])
        self.dv, self.loaded, self.t2_ready, self.stored, self.init = (
            sem(n) for n in ("ffn_dve", "ffn_loaded", "t2_ready", "t2_stored", "ffn_init"))

    def init_dve(self, dve):
        self.nc.vector.memset(self.zf[:], 1.0).then_inc(self.init, 1)
        dve.wait_ge(self.init, 1)

    def load_sp(self, sp, m):
        sp.wait_ge(self.t2_ready, m - self.first)
        sp.dma_start(self.t1[:], token_tiles(self.d.t1, m, self.w)).then_inc(self.loaded, 16)
        sp.dma_start(self.ctx[:], token_tiles(self.d.ctx, m, self.w)).then_inc(self.loaded, 16)

    def store_sp(self, sp, m):
        sp.wait_ge(self.t2_ready, m - self.first + 1)
        sp.dma_start(token_tiles(self.d.t2, m, self.w), self.t2[:]).then_inc(self.stored, 16)

    def vec(self, i):
        return self.r.vecs[:, i:i + 1, :].to_broadcast([P, self.w, P])

    def first_dve(self, dve, n):
        nc, m, r, w = self.nc, self.misc, self.r, self.w
        v = nc.vector
        st = self.st = Steps(dve, self.dv, (n - self.first) * self.DVE_STEPS)
        tiles = m.bank[:, 0:w * P].rearrange("p (t c) -> p t c", t=w)
        m.dve_take(dve)
        m.dve_give(v.tensor_copy(self.ctx_t[:], m.bank[:, 0:w * P]))
        dve.wait_ge(self.loaded, (n - self.first + 1) * 32)
        layer_norm(nc, st, self.xn[:], self.t1[:], self.tmp[:], self.stat, w, P, 1e-5)
        m.dve_take(dve)
        st.link(v.tensor_tensor(self.y[:], tiles, self.vec(0), ALU.add))
        st.link(v.tensor_tensor(self.y[:], self.y[:], self.xn[:], ALU.add))
        layer_norm(nc, st, self.x1[:], self.y[:], self.tmp[:], self.stat, w, P, 1e-5, r.vecs[:, 2, :], r.vecs[:, 3, :])
        z = [q[:] for q in self.z]
        st.link(v.tensor_copy(z[0], self.x1[:, :, 0:HD]))
        cosine(nc, st, *z)
        ry = r.cos_ry[:].rearrange("p (o w) -> p o w", o=1).to_broadcast([P, w, HD])
        m.dve_give(v.tensor_tensor(self.zf[:, :, 0:HD], z[0], ry, ALU.mult))

    def second_dve(self, dve, n):
        nc, m, r, st, w = self.nc, self.misc, self.r, self.st, self.w
        v = nc.vector
        tiles = m.bank[:, 0:w * P].rearrange("p (t c) -> p t c", t=w)
        m.dve_take(dve)
        m.dve_give(v.tensor_copy(self.zf_t[:], m.bank[0:HD + 1, 0:w * P]))
        for c in range(0, 4, self.chunks):
            m.dve_take(dve)
            m.dve_give(v.tensor_scalar(self.h_t[:, c:c + self.chunks, :].rearrange("p c t -> p (c t)"), m.bank[:], 0.0, None, ALU.max))
        m.dve_take(dve)
        m.dve_give(v.tensor_tensor(self.y[:], tiles, self.vec(1), ALU.add))
        m.dve_wait_given(dve)
        st.link(v.tensor_tensor(self.y[:], self.y[:], self.x1[:], ALU.add))
        layer_norm(nc, st, self.xn[:], self.y[:], self.tmp[:], self.stat, w, P, 1e-5, r.vecs[:, 4, :], r.vecs[:, 5, :])
        dve.wait_ge(self.stored, (n - self.first) * 16)
        v.tensor_tensor(self.t2[:], self.xn[:], self.t1[:], ALU.add).then_inc(self.t2_ready, 1)
        assert st.n == self.DVE_STEPS, st.n

    def item_pe(self, pe, n, i):
        nc, m, r, w = self.nc, self.misc, self.r, self.w
        T = nc.tensor
        m.pe_take(pe)
        if i == 0:
            pe.wait_ge(self.loaded, (n - self.first + 1) * 32)
            for t in range(w):
                last = T.transpose(m.bank[:, t * P:(t + 1) * P], self.ctx[:, t, :], r.ident[:])
        elif i == 1:
            for t in range(w):
                last = T.matmul(m.bank[:, t * P:(t + 1) * P], self.ctx_t[:, t * P:(t + 1) * P], r.combw[:], start=True, stop=True)
        elif i == 2:
            for t in range(w):
                last = T.transpose(m.bank[0:HD + 1, t * P:(t + 1) * P], self.zf[:, t, :], r.ident[:])
        elif i < self.items - 1:
            for c in range(self.chunks):
                ffn = (self.chunks * (i - 3) + c) * P
                for t0 in range(0, w * P, 512):
                    t1 = min(t0 + 512, w * P)
                    last = T.matmul(m.bank[:, c * w * P + t0:c * w * P + t1], r.w1[:, ffn:ffn + P], self.zf_t[:, t0:t1], start=True, stop=True)
        else:
            for t in range(w):
                for c in range(4):
                    last = T.matmul(m.bank[:, t * P:(t + 1) * P], self.h_t[:, c, t * P:(t + 1) * P], r.w2[:, c, :],
                                    start=(c == 0), stop=(c == 3))
        m.pe_give(last)


def stage_main(nc, d, r, stack):
    misc = Misc(stack.enter_context(nc.psum_tensor("misc", [P, 512], F32)),
                stack.enter_context(nc.semaphore("misc_full")), stack.enter_context(nc.semaphore("misc_free")))
    conv, at = ConvStep(nc, d, r, stack, misc), AttnStep(nc, d, r, stack, misc)
    ffn = FfnStep(
        nc, d, r, stack, misc, 2, 0,
        {"f_xn": conv.xn, "f_x1": conv.ph, "f_y": conv.tmp, "f_tmp": conv.tmp2,
         "f_h_t": conv.val_t[:, 0:4 * 2 * P].rearrange("p (c t) -> p c t", c=4)})
    LAST = PAIRS - QPAIRS
    ffn4 = FfnStep(nc, d, r, stack, misc, 4, (LAST - LAG) // 2, within(*conv.corners))
    block = stack.enter_context(nc.Block())
    ctx_there = stack.enter_context(nc.semaphore("ctx_there"))
    QUADRUPLES = IMAGES * QUADS
    SEGMENTS, at_misc = [], QPAIRS * 2
    for q0, q1 in ((0, LAG // QPAIRS), (LAG // QPAIRS, (PAIRS - LEAD) // QPAIRS), ((PAIRS - LEAD) // QPAIRS, QUADRUPLES - 1), (QUADRUPLES - 1, QUADRUPLES)):
        has_conv, has_ffn, follows = q1 <= (PAIRS - LEAD) // QPAIRS, q0 >= LAG // QPAIRS, q1 < QUADRUPLES
        per = 2 + 8 * has_conv + (0 if not has_ffn else ffn.items if follows else 2 * ffn4.items) + 2 * follows
        SEGMENTS.append((q0, q1, has_conv, has_ffn, follows, at_misc - q0 * QPAIRS * per, per))
        at_misc += (q1 - q0) * QPAIRS * per

    @block.sync
    def _(sp):
        at.load_q(sp, 0)
        sp.sem_inc(at.ctx_stored[1], 16)
        for q0, q1, has_conv, has_ffn, follows, _, _ in SEGMENTS:
            if has_ffn and not follows:
                sp.wait_ge(conv.stored, (PAIRS - LEAD) * 48)
                for s in range(2):
                    sp.wait_ge(conv.gathered[s], (PAIRS - LEAD + 1) * (16 * TAPS))
            with sp.Fori(q0, q1) as qd:
                if follows:
                    if has_conv:
                        sp.wait_ge(conv.stored, qd * (QPAIRS * 48))
                    else:
                        sp.wait_ge(conv.stored, (PAIRS - LEAD) * 48)
                    at.load_q(sp, qd + 1)
                with sp.Fori(0, QPAIRS) as p:
                    n = qd * QPAIRS + p
                    if has_conv:
                        conv.load_sp(sp, n + LEAD)
                        conv.store_sp(sp, n + LEAD)
                    if has_ffn and not follows:
                        for s in range(2):
                            sp.wait_ge(at.ctx_stored[s], n * 16 + 16 * s)
                            sp.sem_inc(ctx_there, 1)
                        m = (LAST - LAG) // 2 + 2 * (n - LAST)
                        ffn4.load_sp(sp, m)
                        ffn4.store_sp(sp, m)
                        ffn4.load_sp(sp, m + 1)
                    elif has_ffn:
                        for s in range(2):
                            sp.wait_ge(at.ctx_stored[s], n * 16 - 32 + 16 * s)
                            sp.sem_inc(ctx_there, 1)
                        ffn.load_sp(sp, n - LAG)
                    at.store_ctx(sp, 2 * n, 0)
                    if has_ffn and follows:
                        ffn.store_sp(sp, n - LAG)
                    elif has_ffn:
                        ffn4.store_sp(sp, m + 1)
                    at.store_ctx(sp, 2 * n + 1, 1)
        for s in range(2):
            sp.wait_ge(at.ctx_stored[s], (PAIRS + s) * 16)
        sp.wait_ge(conv.stored, (PAIRS - LEAD) * 48)
        sp.wait_ge(ffn.stored, (LAST - LAG) * 16)
        sp.wait_ge(ffn4.stored, 2 * QPAIRS * 16)

    GATHERS = {4: ((0, 0, 2),), 5: ((0, 2, 3),), 6: ((0, 3, 9),), 13: ((1, 6, 9),)}
    GATHERS.update({7 + k: ((1, k, k + 1),) for k in range(6)})

    @block.gpsimd
    def _(pool):
        for s in range(2):
            conv.gather_pool(pool, LEAD, s, range(TAPS))
        for has_conv, n0, n1 in ((True, 0, PAIRS - LEAD), (False, PAIRS - LEAD, PAIRS)):
            with pool.Fori(n0, n1) as n:
                for m in range(at.SPLITS):
                    at.split_pool(pool, n, m)
                    for s, k0, k1 in GATHERS.get(m, ()) if has_conv else ():
                        conv.gather_pool(pool, n + LEAD + 1, s, range(k0, k1))

    @block.scalar
    def _(act):
        act.sem_inc(at.exp_done, at.SC)
        with act.Fori(0, PAIRS // 4) as i:
            for s in range(4):
                at.pair_act(act, 4 * i + s)

    @block.vector
    def _(dve):
        dve.sem_inc(misc.free, 1)
        dve.sem_inc(conv.val_ready, 2)
        for s in range(2):
            conv.stage_dve(dve, LEAD, s)
        at.init_dve(dve)
        ffn.init_dve(dve)
        with dve.Fori(0, QPAIRS) as p:
            misc.start(p * 2)
            at.stage_dve(dve, 0, p)
        at.unit_dve(0, 0)
        for q0, q1, has_conv, has_ffn, follows, misc0, per in SEGMENTS:
            if has_ffn and not follows:
                for s in range(2):
                    dve.wait_ge(conv.gathered[s], (PAIRS - LEAD + 1) * (16 * TAPS))
                ffn4.init_dve(dve)
            with dve.Fori(q0, q1) as qd:
                at.switch_dve(dve, qd)
                with dve.Fori(0, QPAIRS) as p:
                    n = qd * QPAIRS + p
                    misc.start(n * per + misc0)
                    at.finish_dve(dve, 2 * n, n, 1, 2 * n + 1)
                    if has_conv:
                        st = Steps(dve, conv.dv, n * conv.STEPS)
                        for s in range(2):
                            conv.sample_dve(dve, n + LEAD, s, st)
                        for s in range(2):
                            conv.product_dve(dve, n + LEAD, s)
                        conv.ring_dve(dve, n + LEAD, st)
                    if has_ffn and not follows:
                        m = (LAST - LAG) // 2 + 2 * (n - LAST)
                        ffn4.first_dve(dve, m)
                        ffn4.second_dve(dve, m)
                    at.finish_dve(dve, 2 * n + 1, n, 0, 2 * n + 2)
                    if has_ffn and follows:
                        ffn.first_dve(dve, n - LAG)
                        ffn.second_dve(dve, n - LAG)
                    elif has_ffn:
                        ffn4.first_dve(dve, m + 1)
                        ffn4.second_dve(dve, m + 1)
                    if follows:
                        at.stage_dve(dve, qd + 1, p)
                    assert misc.d == per
        misc.start(at_misc)
        at.finish_dve(dve, 2 * PAIRS, PAIRS, 1)

    @block.tensor
    def _(pe):
        with pe.Fori(0, QPAIRS) as p:
            misc.start(p * 2)
            for k in range(2):
                at.stage_pe(pe, 0, p, k)
        pe.sem_inc(at.pv_done, at.PV_START)
        pe.sem_inc(at.low_used, 2)
        at.first_scores(pe, 0, 1)
        for q0, q1, has_conv, has_ffn, follows, misc0, per in SEGMENTS:
            with pe.Fori(q0, q1) as qd:
                with pe.Fori(0, QPAIRS) as p:
                    n = qd * QPAIRS + p
                    misc.start(n * per + misc0)
                    bg = {6: lambda: at.finish_pe(pe, 2 * n), 70: lambda: at.finish_pe(pe, 2 * n + 1)}
                    if has_ffn and not follows:
                        m = (LAST - LAG) // 2 + 2 * (n - LAST)
                        for i, k in enumerate((20, 23, 40, 43, 45, 47, 49, 52)):
                            bg[k] = lambda i=i: ffn4.item_pe(pe, m, i)
                        for i, k in enumerate((75, 78, 95, 98, 100, 102, 104, 107)):
                            bg[k] = lambda i=i: ffn4.item_pe(pe, m + 1, i)
                    elif has_ffn:
                        for i, k in enumerate((73, 76, 94, 97, 100, 103)):
                            bg[k] = lambda i=i: ffn.item_pe(pe, n - LAG, i)
                    if follows:
                        bg[115] = lambda: at.stage_pe(pe, qd + 1, p, 0)
                        bg[118] = lambda: at.stage_pe(pe, qd + 1, p, 1)
                    if has_conv:
                        for s, k0 in ((0, 28), (1, 36)):
                            for item, dk in zip(conv.items_pe(pe, n + LEAD, s), (0, 2, 4, 5, 6, 7)):
                                bg[k0 + dk] = item
                    at.pair_pe(pe, n, bg, (n + 1) // QPAIRS + 1 if follows else QUADRUPLES)
                    assert misc.p == per
        misc.start(at_misc)
        at.finish_pe(pe, 2 * PAIRS)


def stage_ffn_last(nc, d, r, stack):
    W = 8
    FIRST = (2 * (PAIRS - QPAIRS - LAG) + 8 * QPAIRS) // W
    ROUNDS = 2 * PAIRS // W - FIRST
    misc = Misc(stack.enter_context(nc.psum_tensor("misc_last", [P, W * P], F32)),
                stack.enter_context(nc.semaphore("misc_last_full")), stack.enter_context(nc.semaphore("misc_last_free")))
    ffn = FfnStep(nc, d, r, stack, misc, W, FIRST)
    block = stack.enter_context(nc.Block())

    @block.sync
    def _(sp):
        with sp.Fori(FIRST, FIRST + ROUNDS) as n:
            ffn.load_sp(sp, n)
            ffn.store_sp(sp, n)
        sp.wait_ge(ffn.stored, ROUNDS * 16)

    @block.vector
    def _(dve):
        dve.sem_inc(misc.free, 1)
        ffn.init_dve(dve)
        with dve.Fori(FIRST, FIRST + ROUNDS) as n:
            misc.start((n - FIRST) * ffn.items)
            ffn.first_dve(dve, n)
            ffn.second_dve(dve, n)

    @block.tensor
    def _(pe):
        with pe.Fori(FIRST, FIRST + ROUNDS) as n:
            misc.start((n - FIRST) * ffn.items)
            for i in range(ffn.items):
                ffn.item_pe(pe, n, i)



EXPERTS_AT_ONCE = 4
SLOTS = 2


def stage_experts(nc, d, ident, stack):
    sb = lambda n, s, t=F32: stack.enter_context(nc.sbuf_tensor(n, s, t))
    ps = lambda n: stack.enter_context(nc.psum_tensor(n, [P, 512], F32))
    sem = lambda n: stack.enter_context(nc.semaphore(n))
    DUOS, CHUNKS = IMAGES // 2, TOK // 512
    xn = [sb(f"xn_tok{i}", [P, TILES, P]) for i in range(2)]
    big, xn_t, logits, s_t = sb("e_big", [P, TOK]), sb("xn_ch", [P, TOK]), sb("logits", [P, TOK]), sb("s_tok", [P, TILES, P])
    sel = [sb(f"selected{i}", [P, TOK]) for i in range(DUOS)]
    rsqrt_tmp = sb("e_rsqrt", [P, TILES])
    bn, mv = sb("e_bn", [P, TILES, 6]), sb("e_mv", [P, TILES, 2])
    rstd, shift, stat = [[sb(f"e_{n}{i}", [P, TILES]) for i in range(2)] for n in ("rstd", "shift", "stat")]
    top, nmax, total, share = sb("top", [P, TOPK]), sb("nmax", [P, 1]), sb("total", [P, 1]), sb("share", [P, 1])
    gatew, gateb = sb("gatew", [P, NEXP]), sb("gateb", [P, 1])
    b1, b2, b1_t, b2_t = sb("b1", [NEXP, 512]), sb("b2", [NEXP, P]), sb("b1_t", [P, 4, NEXP]), sb("b2_t", [P, NEXP])
    w1 = [sb(f"ew1_{i}", [P, EXPERTS_AT_ONCE, 512]) for i in range(SLOTS)]
    w2 = [sb(f"ew2_{i}", [P, EXPERTS_AT_ONCE, 4, P]) for i in range(SLOTS)]
    pooled, pooled_g = sb("pooled", [P, NEXP, IMAGES]), [sb(f"pooled_g{i}", [P, EXPERTS_AT_ONCE, IMAGES]) for i in range(SLOTS)]
    hs = [sb(f"hs{i}", [P, 512]) for i in range(SLOTS)]
    hb = [sb(f"hb{i}", [P, 4, EXPERTS_AT_ONCE, IMAGES]) for i in range(SLOTS)]
    hg = [sb(f"hg{i}", [P, 4, EXPERTS_AT_ONCE, IMAGES]) for i in range(SLOTS)]
    os = [sb(f"os{i}", [P, P]) for i in range(SLOTS)]
    out_t, out_e = sb("out_t", [P, IMAGES, NEXP]), [sb(f"out_e{i}", [P, P]) for i in range(DUOS)]
    y = [sb(f"y{i}", [P, 512]) for i in range(2)]
    ps_t, ps_l = [ps(f"eps_t{i}") for i in range(2)], [ps(f"eps_l{i}") for i in range(2)]
    ps_p, ps_h, ps_o, ps_b = ps("eps_p"), ps("eps_h"), ps("eps_o"), ps("eps_b")
    (consts, biases, tr_full, tr_free, lg_full, lg_free, xn_ready, ex_ready, s_ready, st_full, pool_full, pool_free, top_ready,
     dv, bias_full, bias_done, pg_ready, h_full, hs_ready, ht_full, hb_ready, hg_ready, o_full, os_ready, ot_full, o_done, oe_full,
     oe_done, y_full, y_free, cleared, ln_ready) = (
        sem(n) for n in ("e_consts", "e_biases", "e_tr_full", "e_tr_free", "lg_full", "lg_free", "xn_ready", "ex_ready", "s_ready",
                         "st_full", "pool_full", "pool_free", "top_ready", "e_dve", "bias_full", "bias_done", "pg_ready", "h_full",
                         "hs_ready", "ht_full", "hb_ready", "hg_ready", "o_full", "os_ready", "ot_full", "o_done", "oe_full",
                         "oe_done", "y_full", "y_free", "e_cleared", "ln_ready"))
    x_in = [sem(f"e_x_in{i}") for i in range(2)]
    w_in = [sem(f"w_in{i}") for i in range(SLOTS)]
    y_out = [sem(f"y_out{i}") for i in range(2)]
    NG = NEXP // EXPERTS_AT_ONCE
    block = stack.enter_context(nc.Block())

    tokens = lambda b: d.t2[b * TOK:(b + 1) * TOK, :].rearrange("(t p) c -> p t c", p=P)

    def stores(sp, b):
        for c in range(CHUNKS):
            sp.wait_ge(y_free, b * CHUNKS + c + 1)
            sp.dma_start(d.out[b, :, c * 512:(c + 1) * 512], y[c % 2][:]).then_inc(y_out[c % 2], 16)

    @block.sync
    def _(sp):
        sp.dma_start(gatew[:], d.gatew).then_inc(consts, 16)
        sp.dma_start(gateb[:], d.gateb).then_inc(consts, 16)
        for b in range(2):
            sp.dma_start(xn[b][:], tokens(b)).then_inc(x_in[b], 16)
        sp.dma_start(b1[:], d.ew1[:, P:P + 1, :].rearrange("e o h -> (e o) h")).then_inc(biases, 16)
        sp.dma_start(b2[:], d.ew2[:, 512:513, :].rearrange("e o h -> (e o) h")).then_inc(biases, 16)

        def weights(g, s):
            e = bass.ds(g * EXPERTS_AT_ONCE, EXPERTS_AT_ONCE)
            sp.dma_start(w1[s][:], d.ew1[e, 0:P, :].rearrange("e p h -> p e h")).then_inc(w_in[s], 16)
            for x in range(EXPERTS_AT_ONCE):
                sp.dma_start(w2[s][:, x], d.ew2[bass.ds(g * EXPERTS_AT_ONCE + x, 1), 0:512, :].rearrange("o (c p) h -> p (o c) h", p=P)).then_inc(w_in[s], 16)

        for g in range(SLOTS):
            weights(g, g)
        for b in range(2, IMAGES):
            sp.wait_ge(pool_full, b - 1)
            sp.dma_start(xn[b % 2][:], tokens(b)).then_inc(x_in[b % 2], 16)
        with sp.Fori(1, NG // SLOTS) as i:
            for s in range(SLOTS):
                sp.wait_ge(o_full, (i - 1) * SLOTS + s + 1)
                weights(i * SLOTS + s, s)
        for b in range(IMAGES):
            sp.wait_ge(pool_full, IMAGES) if b < 2 else sp.wait_ge(y_full, (b - 1) * CHUNKS)
            sp.dma_start(xn[b % 2][:], tokens(b)).then_inc(x_in[b % 2], 16)
            if b:
                stores(sp, b - 1)
        stores(sp, IMAGES - 1)
        for i in range(2):
            sp.wait_ge(y_out[i], IMAGES * CHUNKS // 2 * 16)

    @block.vector
    def _(dve):
        v = nc.vector
        st = Steps(dve, dv)
        for ps in (ps_h, ps_o):
            v.memset(ps[:], 0.0).then_inc(cleared, 1)
        for duo in range(DUOS):
            for i in range(2):
                dve.wait_ge(x_in[i], (duo + 1) * 16)
                for t in range(TILES):
                    last = v.bn_stats(bn[:, t, :], xn[i][:, t, :])
                st.link(last)
                for t in range(TILES):
                    last = v.bn_aggr(mv[:, t, :], bn[:, t, :])
                st.link(last)
                st.link(v.tensor_scalar(stat[i][:], mv[:, :, 1], 1e-5, None, ALU.add))
                rsqrt(nc, st, rstd[i][:], stat[i][:], shift[i][:], rsqrt_tmp[:])
                v.scalar_tensor_tensor(out=shift[i][:], in0=mv[:, :, 0], scalar=-1.0, in1=rstd[i][:], op0=ALU.mult, op1=ALU.mult).then_inc(ln_ready, 1)
                dve.wait_ge(ln_ready, 2 * duo + i + 1)
            dve.wait_ge(lg_free, 2 * CHUNKS * (duo + 1))
            st.link(v.max(top[:], logits[:]))
            v.tensor_scalar(nmax[:], top[:, 0:1], -1.0, None, ALU.mult).then_inc(top_ready, 1)
            st.link(v.match_replace(big[:], top[:], logits[:], -3.0e38))
            st.link(v.tensor_tensor(big[:], big[:], logits[:], ALU.not_equal))
            dve.wait_ge(ex_ready, duo + 1)
            st.link(v.reciprocal(share[:], total[:]))
            v.scalar_tensor_tensor(out=sel[duo][:], in0=xn_t[:], scalar=share[:], in1=big[:], op0=ALU.mult, op1=ALU.mult).then_inc(s_ready, 1)
            dve.wait_ge(s_ready, duo + 1)
            for i in range(2):
                b = 2 * duo + i
                dve.wait_ge(pool_full, b + 1)
                v.tensor_copy(pooled[:, :, b:b + 1], ps_p[:, 0:NEXP].rearrange("p (e o) -> p e o", o=1)).then_inc(pool_free, 1)
        dve.wait_ge(pool_free, IMAGES)
        dve.wait_ge(bias_full, 1)
        v.tensor_copy(b1_t[:], ps_b[:, 0:4 * NEXP].rearrange("p (c e) -> p c e", c=4)).then_inc(bias_done, 1)
        v.tensor_copy(b2_t[:], ps_b[:, 4 * NEXP:5 * NEXP]).then_inc(bias_done, 1)
        dve.wait_ge(bias_done, 2)
        with dve.Fori(0, NG // SLOTS) as i:
            for s in range(SLOTS):
                g = i * SLOTS + s
                es = bass.ds(g * EXPERTS_AT_ONCE, EXPERTS_AT_ONCE)
                v.tensor_copy(pooled_g[s][:], pooled[:, es, :]).then_inc(pg_ready, 1)
                dve.wait_ge(ht_full, g + 1)
                bias1 = b1_t[:, :, es].rearrange("p c (e o) -> p c e o", o=1).to_broadcast([P, 4, EXPERTS_AT_ONCE, IMAGES])
                v.tensor_tensor(hb[s][:], ps_t[0][:].rearrange("p (c e b) -> p c e b", c=4, b=32)[:, :, :, 0:IMAGES], bias1, ALU.add).then_inc(hb_ready, 1)
                dve.wait_ge(o_full, g + 1)
                v.tensor_copy(os[s][:], ps_o[:, 0:P]).then_inc(os_ready, 1)
                dve.wait_ge(ot_full, g + 1)
                bias2 = b2_t[:, es].rearrange("p (o e) -> p o e", o=1).to_broadcast([P, IMAGES, EXPERTS_AT_ONCE])
                v.tensor_tensor(out_t[:, :, es], ps_t[1][:, 0:P].rearrange("p (e b) -> p b e", b=32)[:, 0:IMAGES, :], bias2, ALU.add).then_inc(o_done, 1)
        for duo in range(DUOS):
            dve.wait_ge(oe_full, duo + 1)
            v.tensor_copy(out_e[duo][:], ps_t[duo][:, 0:P]).then_inc(oe_done, 1)
        for n in range(IMAGES * CHUNKS):
            dve.wait_ge(y_full, n + 1)
            if n >= 2:
                dve.wait_ge(y_out[n % 2], n // 2 * 16)
            v.tensor_copy(y[n % 2][:], ps_l[n % 2][:]).then_inc(y_free, 1)

    @block.scalar
    def _(act):
        n = 0

        def normalise(duo, i):
            act.wait_ge(ln_ready, 2 * duo + i + 1)
            for t in range(TILES):
                last = nc.scalar.activation(xn[i][:, t, :], xn[i][:, t, :], ACT.Identity, scale=rstd[i][:, t:t + 1], bias=shift[i][:, t:t + 1])
            last.then_inc(xn_ready, 1)

        for duo in range(DUOS):
            normalise(duo, 0)
            for i in range(2):
                for g in range(CHUNKS):
                    act.wait_ge(tr_full, n + 1)
                    if g == 0 and i == 0 and duo:
                        act.wait_ge(s_ready, duo)
                    if g == 0 and i == 1:
                        act.wait_ge(lg_full, 2 * CHUNKS * duo + CHUNKS)
                    nc.scalar.copy(xn_t[:, g * 512:(g + 1) * 512], ps_t[n % 2][:]).then_inc(tr_free, 1)
                    n += 1
                if i == 0:
                    normalise(duo, 1)
                half = slice(NEXP * i, NEXP * i + NEXP)
                act.wait_ge(consts, 32)
                for c in range(CHUNKS):
                    act.wait_ge(lg_full, 2 * CHUNKS * duo + CHUNKS * i + c + 1)
                    nc.scalar.activation(logits[half, c * 512:(c + 1) * 512], ps_l[c % 2][half, :], ACT.Identity,
                                         bias=gateb[half, :]).then_inc(lg_free, 1)
            act.wait_ge(top_ready, duo + 1)
            act.wait_ge(lg_full, 2 * CHUNKS * (duo + 1))
            nc.scalar.activation(xn_t[:], logits[:], ACT.Exp, bias=nmax[:], accum_out=total[:]).then_inc(ex_ready, 1)
            for g in range(CHUNKS):
                act.wait_ge(tr_full, n + 1)
                nc.scalar.copy(s_t[:, 4 * g:4 * g + 4, :].rearrange("p t c -> p (t c)"), ps_t[n % 2][:]).then_inc(tr_free, 1)
                n += 1
        with act.Fori(0, NG // SLOTS) as i:
            for s in range(SLOTS):
                act.wait_ge(h_full, i * SLOTS + s + 1)
                nc.scalar.copy(hs[s][:], ps_h[:]).then_inc(hs_ready, 1)
                act.wait_ge(hb_ready, i * SLOTS + s + 1)
                nc.scalar.activation(hg[s][:], hb[s][:], ACT.Gelu).then_inc(hg_ready, 1)

    @block.tensor
    def _(pe):
        T = nc.tensor
        n = 0
        for duo in range(DUOS):
            for i in range(2):
                pe.wait_ge(xn_ready, 2 * duo + i + 1)
                for g in range(CHUNKS):
                    if n >= 2:
                        pe.wait_ge(tr_free, n - 1)
                    for j in range(4):
                        last = T.transpose(ps_t[n % 2][:, j * P:(j + 1) * P], xn[i][:, 4 * g + j, :], ident[:])
                    last.then_inc(tr_full, 1)
                    n += 1
                for c in range(CHUNKS):
                    k = 2 * CHUNKS * duo + CHUNKS * i + c
                    pe.wait_ge(tr_free, n - CHUNKS + c + 1)
                    if k == 0:
                        pe.wait_ge(consts, 32)
                    if k >= 2:
                        pe.wait_ge(lg_free, k - 1)
                    T.matmul(ps_l[c % 2][NEXP * i:NEXP * (i + 1), :], gatew[:], xn_t[:, c * 512:(c + 1) * 512], start=True, stop=True).then_inc(lg_full, 1)
            pe.wait_ge(s_ready, duo + 1)
            for g in range(CHUNKS):
                pe.wait_ge(tr_free, n - 1)
                for j in range(4):
                    t = 4 * g + j
                    last = T.transpose(ps_t[n % 2][:, j * P:(j + 1) * P], sel[duo][:, t * P:(t + 1) * P], ident[:])
                last.then_inc(tr_full, 1)
                n += 1
            pe.wait_ge(tr_free, n)
            for i in range(2):
                b = 2 * duo + i
                if b:
                    pe.wait_ge(pool_free, b)
                for t in range(TILES):
                    last = T.matmul(ps_p[:, 0:NEXP], xn[i][:, t, :], s_t[:, t, NEXP * i:NEXP * (i + 1)], start=(t == 0), stop=(t == TILES - 1))
                last.then_inc(pool_full, 1)
        pe.wait_ge(cleared, 2)
        pe.wait_ge(biases, 32)
        for c in range(4):
            T.transpose(ps_b[:, c * NEXP:(c + 1) * NEXP], b1[:, c * P:(c + 1) * P], ident[0:NEXP, 0:NEXP])
        T.transpose(ps_b[:, 4 * NEXP:5 * NEXP], b2[:], ident[0:NEXP, 0:NEXP]).then_inc(bias_full, 1)
        with pe.Fori(0, NG // SLOTS) as i:
            for s in range(SLOTS):
                g = i * SLOTS + s
                pe.wait_ge(w_in[s], (i + 1) * 16 * (1 + EXPERTS_AT_ONCE))
                pe.wait_ge(pg_ready, g + 1)
                pe.wait_ge(hs_ready, g)
                for e in range(EXPERTS_AT_ONCE):
                    last = T.matmul(ps_h[32 * e:32 * e + IMAGES, :], pooled_g[s][:, e, :], w1[s][:, e, :], start=True, stop=True)
                last.then_inc(h_full, 1)
                pe.wait_ge(hs_ready, g + 1)
                for c in range(4):
                    last = T.transpose(ps_t[0][:, c * P:(c + 1) * P], hs[s][:, c * P:(c + 1) * P], ident[:])
                last.then_inc(ht_full, 1)
                pe.wait_ge(hg_ready, g + 1)
                for c in range(4):
                    for e in range(EXPERTS_AT_ONCE):
                        last = T.matmul(ps_o[32 * e:32 * e + IMAGES, 0:P], hg[s][:, c, e, :], w2[s][:, e, c, :], start=(c == 0), stop=(c == 3))
                last.then_inc(o_full, 1)
                pe.wait_ge(os_ready, g + 1)
                pe.wait_ge(o_done, g)
                T.transpose(ps_t[1][:, 0:P], os[s][:], ident[:]).then_inc(ot_full, 1)
        pe.wait_ge(o_done, NG)
        for duo in range(DUOS):
            T.transpose(ps_t[duo][:, 0:P], out_t[:, 2 * duo:2 * duo + 2, :].rearrange("p b e -> p (b e)"), ident[:]).then_inc(oe_full, 1)
        pe.wait_ge(oe_done, DUOS)
        for b in range(IMAGES):
            pe.wait_ge(x_in[b % 2], (DUOS + b // 2 + 1) * 16)
            half = slice(NEXP * (b % 2), NEXP * (b % 2 + 1))
            for c in range(CHUNKS):
                n = b * CHUNKS + c
                if n >= 2:
                    pe.wait_ge(y_free, n - 1)
                T.matmul(ps_l[c % 2][:], out_e[b // 2][half, :], sel[b // 2][half, c * 512:(c + 1) * 512], start=True, stop=False)
                for j in range(4):
                    last = T.matmul(ps_l[c % 2][:, j * P:(j + 1) * P], xn[b % 2][:, 4 * c + j, :], ident[:], start=False, stop=(j == 3))
                last.then_inc(y_full, 1)


class Views:

    def __init__(self, nc, arrays, kinds):
        view = {k: nc.dram_tensor("in_" + k, v.shape, mybir.dt.from_np(v.dtype), kind="ExternalInput").ap()
                for k, v in arrays.items()}
        self.x, self.x_tok, self.offw, self.offb, self.dcnw = (view[k] for k in ("x", "x_tok", "offw", "offb", "dcnw"))
        self.base, self.gmat, self.gatew, self.gateb = (view[k] for k in ("base", "gmat", "gatew", "gateb"))
        self.ew1, self.ew2 = view["ew1"], view["ew2"]
        self.shared = {k: view[k] for k in SHARED}
        inner = lambda name, shape: nc.dram_tensor(name, shape, F32, kind=kinds.get(name, "Internal")).ap()
        self.table = inner("table", (IMAGES * TROWS, 4 * P))
        self.t1 = inner("t1", (IMAGES * TOK, CH))
        self.q = inner("q", (QUADS, IMAGES * TOK, 4 * HD))
        self.ctx = inner("ctx", (IMAGES * TOK, CH))
        self.t2 = inner("t2", (IMAGES * TOK, CH))
        self.out = nc.dram_tensor("out", (IMAGES, CH, TOK), F32, kind="ExternalOutput").ap()


class Shared:

    def __init__(self, nc, stack, ident):
        sb = lambda n, s, t=F32: stack.enter_context(nc.sbuf_tensor(n, s, t))
        self.ident = ident
        self.idx = sb("idx", [P, IMAGES * TILES * TAPS], I32)
        self.wts = sb("wts", [P, IMAGES * TILES, TAPS, 4])
        self.ident16 = sb("ident16", [P, P], F16)
        self.image_row, self.theta, self.dcnw = sb("image_row", [P, IMAGES]), sb("theta", [P, P]), sb("dcnw", [P, TAPS, P])
        self.combw, self.vecs, self.w1 = sb("combw", [P, P]), sb("vecs", [P, 6, P]), sb("w1", [HD + 1, FFN])
        self.w2, self.cos_ry = sb("w2", [P, 4, P]), sb("cos_ry", [P, HD])


def host_layout(inputs):
    a = {k: np.asarray(v) for k, v in inputs.items()}
    rep = lambda v: np.tile(v.reshape(1, -1), (P, 1))
    x = a["x"].reshape(IMAGES, CH, TOK)
    p = np.arange(P)
    tile_y = 2 * np.arange(TILES)[None, :, None] + (p // SIDE)[:, None, None] + (np.arange(TAPS) // 3)[None, None, :]
    tile_x = (p % SIDE)[:, None, None] + 0 * np.arange(TILES)[None, :, None] + (np.arange(TAPS) % 3)[None, None, :]
    out = {
        "x": x,
        "x_tok": x.transpose(0, 2, 1).reshape(IMAGES * TOK, CH),
        "offw": a["L0_conv_offset_w"].reshape(27, CH, TAPS).transpose(1, 2, 0),
        "offb": np.tile(np.pad(a["L0_conv_offset_b"], (0, 5)), 4)[:, None],
        "dcnw": a["L0_conv_dcn_w"].reshape(CH, CH, TAPS).transpose(1, 2, 0),
        "base": np.stack([tile_y, tile_x], 1).astype(np.float32),
        "gmat": np.kron(np.eye(32), np.full((4, 4), 0.25)).astype(np.float32),
        "ident": np.eye(P, dtype=np.float32),
        "image_row": rep(np.arange(IMAGES) * TROWS + MARGIN).astype(np.float32),
        "theta": rep(np.tile(a["L1_attn_rx_theta"], HEADS)),
        "ry": rep(a["L1_attn_ry_theta"]),
        "combw": a["L1_attn_w_comb"].T,
        "vecs": np.stack([rep(a["L1_attn_" + n]) for n in ("b_comb", "b2", "g1", "beta1", "g2", "beta2")], 1),
        "w1": np.concatenate([a["L1_attn_w1"].T, a["L1_attn_b1"][None]], 0),
        "w2": a["L1_attn_w2"].T.reshape(4, P, CH).transpose(1, 0, 2),
        "gatew": a["L1_ffn_gate_w"].T,
        "gateb": np.tile(a["L1_ffn_gate_b"], 2)[:, None],
        "ew1": a["L1_ffn_weight1"],
        "ew2": a["L1_ffn_weight2"],
    }
    return {k: np.ascontiguousarray(v) for k, v in out.items()}


SHARED = ("ident", "image_row", "theta", "dcnw", "combw", "vecs", "w1", "w2", "ry")


def build(nc, arrays, stages=("offsets", "conv", "main", "experts"), kinds={}):
    d = Views(nc, arrays, kinds)
    with ExitStack() as whole:
        ident = whole.enter_context(nc.sbuf_tensor("ident", [P, P], F32))
        with ExitStack() as body:
            r = Shared(nc, body, ident)
            stage_constants(nc, d, r, body)
            if "offsets" in stages:
                with ExitStack() as st:
                    stage_offsets(nc, d, r, st)
            if "conv" in stages:
                with ExitStack() as st:
                    stage_conv_first(nc, d, r, st)
            if "main" in stages:
                with ExitStack() as st:
                    stage_main(nc, d, r, st)
                with ExitStack() as st:
                    stage_ffn_last(nc, d, r, st)
        if "experts" in stages:
            with ExitStack() as st:
                stage_experts(nc, d, ident, st)


def stage_constants(nc, d, r, stack):
    places = (r.ident, r.image_row, r.theta, r.dcnw, r.combw, r.vecs, r.w1, r.w2, r.cos_ry)
    scratch = [stack.enter_context(nc.sbuf_tensor(f"ry{i}", [P, HD], F32)) for i in range(3)]
    with ExitStack() as s:
        loaded, dv = (s.enter_context(nc.semaphore(n)) for n in ("shared_loaded", "shared_dve"))
        block = s.enter_context(nc.Block())

        @block.sync
        def _(sp):
            for place, name in zip(places, SHARED):
                sp.dma_start(place[:], d.shared[name]).then_inc(loaded, 16)
            sp.wait_ge(loaded, 16 * len(places))

        @block.vector
        def _(dve):
            dve.wait_ge(loaded, 16 * len(places))
            st = Steps(dve, dv)
            st.link(nc.vector.tensor_copy(r.ident16[:], r.ident[:]))
            cosine(nc, st, r.cos_ry[:], *(q[:] for q in scratch))


def kernel(**inputs):
    from concourse import bacc
    from concourse.bass_utils import run_bass_kernel_spmd

    arrays = host_layout(inputs)
    nc = bacc.Bacc("TRN2", target_bir_lowering=False, num_devices=1)
    build(nc, arrays)
    result = run_bass_kernel_spmd(nc, [{"in_" + k: v for k, v in arrays.items()}], core_ids=[0])
    return result.results[0]["out"].reshape(IMAGES, CH, SIDE, SIDE)
```
